# Optimizing a Trainium2 kernel written in Bass

```python
import numpy as np
import jax
import jax.numpy as jnp

def _softmax(x, axis=-1):
    return jax.nn.softmax(x, axis=axis)

def _gelu(x):
    return jax.nn.gelu(x, approximate=True)

def _silu(x):
    return jax.nn.silu(x)

def _sigmoid(x):
    return jax.nn.sigmoid(x)

def _layernorm(x, axis=-1, eps=1e-05):
    m = jnp.mean(x, axis=axis, keepdims=True)
    v = jnp.var(x, axis=axis, keepdims=True)
    return (x - m) / jnp.sqrt(v + eps)

def _scatter_add(tgt, idx, src, axis=0):
    return tgt.at[idx].add(src)

def _segment_sum(src, seg, n):
    return jax.ops.segment_sum(src, seg, n)
kernel_name = 'mk_cond_resid_d4_seqx_r8_8c8696'

def setup_inputs(seed: int=0):
    np.random.seed(seed)
    _w = jnp.asarray

    def _rec_inputs():
        import jax
        import jax.numpy as jnp
        _rk = jax.random.key(seed)
        x = 7.22e-05 + 1 * jax.random.normal(jax.random.fold_in(_rk, 1), (8, 256, 128), jnp.float32)
        _lenS = 256 - jax.random.randint(jax.random.fold_in(_rk, 7), (8,), 0, max(1, 256 // 4) + 1, jnp.int32)
        _lenS2 = 256 - jax.random.randint(jax.random.fold_in(_rk, 8), (8,), 0, max(1, 256 // 4) + 1, jnp.int32)
        cond_8 = jax.random.uniform(jax.random.fold_in(_rk, 11), (8, 8), jnp.float32, 0.0, 0.999837)
        return (x, cond_8)
    x, cond_8 = _rec_inputs()

    def _L0_cond_setup():
        import jax, jax.numpy as jnp
        import numpy as np
        key = jax.random.key(seed)
        k1, k2, k3, k4, k5 = jax.random.split(key, 5)
        B, N, T, O, G = (32, 32, 128, 128, 8)
        x = jax.random.normal(k1, (B, N, T), dtype=jnp.float32)
        y = jax.random.uniform(k2, (B, G), dtype=jnp.float32)
        weight = jax.random.normal(k3, (G, O, T), dtype=jnp.float32) * (1.0 / np.sqrt(T))
        mask = jax.random.uniform(k4, (O, T), dtype=jnp.float32)
        bias = jax.random.normal(k5, (O,), dtype=jnp.float32)
        return {'x': x, 'y': y, 'weight': weight, 'mask': mask, 'bias': bias}
    _L0_cond_all = _L0_cond_setup()
    _L0_cond_in = {k: v for k, v in _L0_cond_all.items() if k in ('weight', 'mask', 'bias')}
    del _L0_cond_all

    def _L1_cond_setup():
        import jax, jax.numpy as jnp
        import numpy as np
        R = 16
        ALPHA = 32.0
        SCALING = ALPHA / R
        key = jax.random.key(seed)
        ks = jax.random.split(key, 6)
        B, T, C, O, E = (16, 1500, 128, 128, 8)
        x = jax.random.normal(ks[0], (B, T, C), dtype=jnp.float32)
        w = jax.random.uniform(ks[1], (B, E), dtype=jnp.float32)
        W_base = jax.random.normal(ks[2], (O, C), dtype=jnp.float32) * 0.02
        b_base = jax.random.normal(ks[3], (O,), dtype=jnp.float32) * 0.02
        As = jax.random.normal(ks[4], (E, R, C), dtype=jnp.float32) * 0.02
        Bs = jax.random.normal(ks[5], (E, O, R), dtype=jnp.float32) * 0.02
        return {'x': x, 'w': w, 'W_base': W_base, 'b_base': b_base, 'As': As, 'Bs': Bs}
    _L1_cond_all = _L1_cond_setup()
    _L1_cond_in = {k: v for k, v in _L1_cond_all.items() if k in ('W_base', 'b_base', 'As', 'Bs')}
    del _L1_cond_all

    def _L2_cond_setup():
        import jax, jax.numpy as jnp
        import numpy as np
        TOP_K = 2
        NUM_MOE_LAYERS = 12

        def _gemma_mlp(x, gate_w, up_w, down_w):
            g = jnp.einsum('bsh,hi->bsi', x, gate_w)
            u = jnp.einsum('bsh,hi->bsi', x, up_w)
            return jnp.einsum('bsi,ih->bsh', jax.nn.gelu(g, approximate=True) * u, down_w)
        key = jax.random.key(seed)
        ks = jax.random.split(key, 8)
        B, S, H, I, E = (32, 32, 128, 512, 8)
        std = 0.02
        return {'x': jax.random.normal(ks[0], (B, S, H), jnp.float32), 'router_logits': jax.random.normal(ks[1], (B, E), jnp.float32), 'skill_gate': jax.random.normal(ks[2], (E, H, I), jnp.float32) * std, 'skill_up': jax.random.normal(ks[3], (E, H, I), jnp.float32) * std, 'skill_down': jax.random.normal(ks[4], (E, I, H), jnp.float32) * std, 'shared_gate': jax.random.normal(ks[5], (H, I), jnp.float32) * std, 'shared_up': jax.random.normal(ks[6], (H, I), jnp.float32) * std, 'shared_down': jax.random.normal(ks[7], (I, H), jnp.float32) * std}
    _L2_cond_all = _L2_cond_setup()
    _L2_cond_in = {k: v for k, v in _L2_cond_all.items() if k in ('skill_gate', 'skill_up', 'skill_down', 'shared_gate', 'shared_up', 'shared_down')}
    del _L2_cond_all

    def _L3_cond_setup():
        import jax, jax.numpy as jnp
        import numpy as np
        B, S, D = (16, 256, 128)
        E, H = (8, 256)
        key = jax.random.key(seed)
        ks = jax.random.split(key, 8)
        scale = 0.02
        x = jax.random.normal(ks[0], (B, S, D), dtype=jnp.float32)
        opcode_onehot = jax.random.uniform(ks[1], (B, E), dtype=jnp.float32)
        W_up = jax.random.normal(ks[2], (E, H, D), dtype=jnp.float32) * scale
        b_up = jnp.zeros((E, H), dtype=jnp.float32)
        W_gate = jax.random.normal(ks[3], (E, H, D), dtype=jnp.float32) * scale
        b_gate = jnp.zeros((E, H), dtype=jnp.float32)
        W_down = jax.random.normal(ks[4], (E, D, H), dtype=jnp.float32) * scale
        b_down = jnp.zeros((E, D), dtype=jnp.float32)
        return {'x': x, 'opcode_onehot': opcode_onehot, 'W_up': W_up, 'b_up': b_up, 'W_gate': W_gate, 'b_gate': b_gate, 'W_down': W_down, 'b_down': b_down}
    _L3_cond_all = _L3_cond_setup()
    _L3_cond_in = {k: v for k, v in _L3_cond_all.items() if k in ('W_up', 'b_up', 'W_gate', 'b_gate', 'W_down', 'b_down')}
    del _L3_cond_all
    return {'x': x, 'cond_8': cond_8, 'L0_cond_weight': _L0_cond_in['weight'], 'L0_cond_mask': _L0_cond_in['mask'], 'L0_cond_bias': _L0_cond_in['bias'], 'L1_cond_W_base': _L1_cond_in['W_base'], 'L1_cond_b_base': _L1_cond_in['b_base'], 'L1_cond_As': _L1_cond_in['As'], 'L1_cond_Bs': _L1_cond_in['Bs'], 'L2_cond_skill_gate': _L2_cond_in['skill_gate'], 'L2_cond_skill_up': _L2_cond_in['skill_up'], 'L2_cond_skill_down': _L2_cond_in['skill_down'], 'L2_cond_shared_gate': _L2_cond_in['shared_gate'], 'L2_cond_shared_up': _L2_cond_in['shared_up'], 'L2_cond_shared_down': _L2_cond_in['shared_down'], 'L3_cond_W_up': _L3_cond_in['W_up'], 'L3_cond_b_up': _L3_cond_in['b_up'], 'L3_cond_W_gate': _L3_cond_in['W_gate'], 'L3_cond_b_gate': _L3_cond_in['b_gate'], 'L3_cond_W_down': _L3_cond_in['W_down'], 'L3_cond_b_down': _L3_cond_in['b_down']}

def reference(x, cond_8, L0_cond_weight, L0_cond_mask, L0_cond_bias, L1_cond_W_base, L1_cond_b_base, L1_cond_As, L1_cond_Bs, L2_cond_skill_gate, L2_cond_skill_up, L2_cond_skill_down, L2_cond_shared_gate, L2_cond_shared_up, L2_cond_shared_down, L3_cond_W_up, L3_cond_b_up, L3_cond_W_gate, L3_cond_b_gate, L3_cond_W_down, L3_cond_b_down):
    import jax
    import jax.numpy as jnp

    def _L0_cond_ref(x, y, weight, mask, bias):
        import jax, jax.numpy as jnp
        import numpy as np
        masked_w = weight * mask[None, :, :]
        w_bot = jnp.einsum('bg,got->bot', y, masked_w)
        return jnp.einsum('bnt,bot->bno', x, w_bot) + bias

    def _L1_cond_ref(x, w, W_base, b_base, As, Bs):
        import jax, jax.numpy as jnp
        import numpy as np
        R = 16
        ALPHA = 32.0
        SCALING = ALPHA / R
        out = jnp.einsum('btc,oc->bto', x, W_base) + b_base
        h = jnp.einsum('btc,erc->bter', x, As)
        lora = jnp.einsum('bter,eor,be->bto', h, Bs, w)
        return out + lora * SCALING

    def _L2_cond_ref(x, router_logits, skill_gate, skill_up, skill_down, shared_gate, shared_up, shared_down):
        import jax, jax.numpy as jnp
        import numpy as np
        TOP_K = 2
        NUM_MOE_LAYERS = 12

        def _gemma_mlp(x, gate_w, up_w, down_w):
            g = jnp.einsum('bsh,hi->bsi', x, gate_w)
            u = jnp.einsum('bsh,hi->bsi', x, up_w)
            return jnp.einsum('bsi,ih->bsh', jax.nn.gelu(g, approximate=True) * u, down_w)
        B = x.shape[0]
        E = skill_gate.shape[0]
        rw = jax.nn.softmax(router_logits.astype(jnp.float32), axis=-1)
        w, sel = jax.lax.top_k(rw, TOP_K)
        w = w / w.sum(axis=-1, keepdims=True)
        w = w.astype(x.dtype)
        scale = 1.0 / NUM_MOE_LAYERS
        w = scale * w + (1.0 - scale) * jax.lax.stop_gradient(w)
        dense_w = jnp.zeros((B, E), x.dtype).at[jnp.arange(B)[:, None], sel].add(w)

        def step(acc, params):
            g, u, d, we = params
            return (acc + we[:, None, None] * _gemma_mlp(x, g, u, d), None)
        out, _ = jax.lax.scan(step, jnp.zeros_like(x), (skill_gate, skill_up, skill_down, dense_w.T))
        out = out + _gemma_mlp(x, shared_gate, shared_up, shared_down)
        return out

    def _L3_cond_ref(x, opcode_onehot, W_up, b_up, W_gate, b_gate, W_down, b_down):
        import jax, jax.numpy as jnp
        import numpy as np
        B, S, D = (16, 256, 128)
        E, H = (8, 256)
        expert = jnp.argmax(opcode_onehot, axis=-1)
        wu, bu = (W_up[expert], b_up[expert])
        wg, bg = (W_gate[expert], b_gate[expert])
        wd, bd = (W_down[expert], b_down[expert])
        up = jnp.einsum('bsd,bhd->bsh', x, wu) + bu[:, None, :]
        gate = jnp.einsum('bsd,bhd->bsh', x, wg) + bg[:, None, :]
        hidden = jax.nn.silu(up) * gate
        out = jnp.einsum('bsh,bdh->bsd', hidden, wd) + bd[:, None, :]
        return out
    x = x + _L0_cond_ref(x, cond_8, L0_cond_weight, L0_cond_mask, L0_cond_bias)
    x = x + _L1_cond_ref(x, cond_8, L1_cond_W_base, L1_cond_b_base, L1_cond_As, L1_cond_Bs)
    x = x + _L2_cond_ref(x, cond_8, L2_cond_skill_gate, L2_cond_skill_up, L2_cond_skill_down, L2_cond_shared_gate, L2_cond_shared_up, L2_cond_shared_down)
    x = x + _L3_cond_ref(x, cond_8, L3_cond_W_up, L3_cond_b_up, L3_cond_W_gate, L3_cond_b_gate, L3_cond_W_down, L3_cond_b_down)
    return x

_drawn_inputs = setup_inputs


def setup_inputs(seed=0):
    import zlib

    import numpy as np

    out = dict(_drawn_inputs(seed))
    spreads = {'L3_cond_b_up': (0.0, 0.8), 'L3_cond_b_gate': (0.0, 0.8), 'L3_cond_b_down': (0.0, 0.322)}
    factors = {'L1_cond_b_base': 4.871,
     'L2_cond_skill_gate': 3.502,
     'L2_cond_skill_up': 3.439,
     'L2_cond_skill_down': 3.378,
     'L3_cond_W_up': 3.686,
     'L3_cond_W_gate': 3.691,
     'L3_cond_W_down': 3.583,
     'L2_cond_shared_gate': 2.737,
     'L2_cond_shared_down': 2.678}
    for name, (base, spread) in spreads.items():
        noise = np.random.default_rng([zlib.crc32(name.encode()), seed]).standard_normal(out[name].shape)
        drawn = base * np.exp(spread * noise) if base else spread * noise
        out[name] = jnp.asarray(drawn.astype(out[name].dtype))
    for name, factor in factors.items():
        out[name] = (out[name] * factor).astype(out[name].dtype)
    return out
```

```python
from contextlib import ExitStack

import numpy as np

import concourse.bass as bass
from concourse import mybir

F32 = mybir.dt.float32
F32R = mybir.dt.float32r
I32 = mybir.dt.int32
ALU = mybir.AluOpType
ACT = mybir.ActivationFunctionType
AX_X = mybir.AxisListType.X

P = 128
B, S, D = 8, 256, 128
E = 8
RANK = 16
LORA_SCALE = 32.0 / RANK
I_MOE = 512
H_L3 = 256
TOKENS = B * S
PAIR = 2 * S
PAIRS = B // 2
SLAB = 3 * 256
SLAB_GU = 512
HALVES = I_MOE // 256
SLABS_EXPERTS = E * HALVES
SLABS_L3 = E
SHARED_AT = (SLABS_EXPERTS + SLABS_L3) * SLAB
SLABS = SLABS_EXPERTS + SLABS_L3 + HALVES
MOE_LAYER_SCALE = 1.0 / 12
TBLK = D // RANK

UNITS_SHARED = PAIRS * 4
UNITS_ROUTED = B * 4
PREPS = UNITS_ROUTED + B
R0 = UNITS_SHARED
T0 = UNITS_SHARED + UNITS_ROUTED
W_SLOTS = 4
DMA = 16

C_BLOCK = 0
C_DELTA = C_BLOCK + E
C_RANK = C_DELTA + RANK
C_IDENT = C_RANK + E
C_COLS = C_IDENT + P


def build(nc, xT, cond, consts, w_l0, lin, vecs, slabs, outT):
    with ExitStack() as ctx:
        def sb(name, shape, dt=F32):
            return ctx.enter_context(nc.sbuf_tensor(name, shape, dt))

        def bank(name):
            return ctx.enter_context(nc.psum_tensor(name, [P, 512], F32))

        def sem(name):
            return ctx.enter_context(nc.semaphore(name))

        w_all = sb("w_all", [P, SLABS * SLAB])
        x_in = sb("x_in", [P, TOKENS])
        cond_sb = sb("cond_sb", [P, B, E])
        const_sb = sb("const_sb", [P, C_COLS])
        w_l0_sb = sb("w_l0_sb", [P, TBLK, P])
        lin_sb = sb("lin_sb", [P, 4, P])
        vec_sb = sb("vec_sb", [P, 2 + 5 * E])
        block_of = const_sb[:, C_BLOCK:C_BLOCK + E]
        delta = const_sb[:, C_DELTA:C_DELTA + RANK]
        rank_e = const_sb[:, C_RANK:C_RANK + E]
        ident = const_sb[:, C_IDENT:C_IDENT + P]
        mask, lora_a, lora_bT, w_baseT = (lin_sb[:, k, :] for k in range(4))
        bias_l0, bias_l1 = vec_sb[:, 0:1], vec_sb[:, 1:2]
        bias_l3 = vec_sb[:, 2:].rearrange("p (k e) -> p k e", e=E)

        cond_blk = sb("cond_blk", [P, B, E])
        cond_row = sb("cond_row", [P, B])
        y_diag = sb("y_diag", [P, B, RANK])
        lora_bw = sb("lora_bw", [P, B, P])
        base_i = sb("base_i", [P, P])
        w0_b = sb("w0_b", [P, B, P])
        r1_b = sb("r1_b", [P, B, P])
        m_b = sb("m_b", [P, B, P])
        c_b = sb("c_b", [P, B])
        x_res = sb("x_res", [P, TOKENS])
        x_hi = sb("x_hi", [P, TOKENS], F32R)
        x_lo = sb("x_lo", [P, TOKENS], F32R)

        top1 = sb("top1", [P, B])
        shifted = sb("shifted", [P, B, E])
        expd = sb("expd", [P, B, E])
        exp_sum = sb("exp_sum", [P, B])
        probs = sb("probs", [P, B, E])
        hit = sb("hit", [P, 2, B, E])
        key = sb("key", [P, B, E])
        first = sb("first", [P, 2, B])
        one_hot = sb("one_hot", [P, 2, B, E])
        rest = sb("rest", [P, B, E])
        top2 = sb("top2", [P, B])
        picked = sb("picked", [P, 2, B, E])
        w_pick = sb("w_pick", [P, 2, B])
        w_sum = sb("w_sum", [P, B])
        w_norm = sb("w_norm", [P, 2, B])
        w_part = sb("w_part", [P, 2, B])
        w_route = sb("w_route", [P, 2 * B])
        slab_at = sb("slab_at", [1, PREPS], I32)
        bias_prod = sb("bias_prod", [P, 5, B, E])
        bias_b = sb("bias_b", [P, 5, B])

        sh_hi = sb("sh_hi", [P, HALVES * SLAB], F32R)
        sh_lo = sb("sh_lo", [P, HALVES * SLAB], F32R)
        w_hi = sb("w_hi", [P, W_SLOTS, SLAB], F32R)
        w_lo = sb("w_lo", [P, W_SLOTS, SLAB], F32R)
        h_act = sb("h_act", [P, 2, 512])
        h_full = sb("h_full", [P, 2, 512])
        h_hi = sb("h_hi", [P, 2, 512], F32R)
        h_lo = sb("h_lo", [P, 2, 512], F32R)

        gate_ps = [bank("gate0"), bank("gate1")]
        up_ps = [bank("up0"), bank("up1")]
        acc_ps = [bank("acc0"), bank("acc1")]
        spare = [bank("spare0"), bank("spare1")]

        d_small, d_lin, d_x, d_shared, d_experts, d_l3 = (
            sem(n) for n in ("d_small", "d_lin", "d_x", "d_shared", "d_experts", "d_l3"))
        d_out = sem("d_out")
        dve_step = sem("dve_step")
        y_ready, bw_ready = sem("y_ready"), sem("bw_ready")
        w0_sum, lora_sum = sem("w0_sum"), sem("lora_sum")
        w0_ready, r1_ready = sem("w0_ready"), sem("r1_ready")
        m_sum, m_ready = sem("m_sum"), sem("m_ready")
        c_sum, c_ready = sem("c_sum"), sem("c_ready")
        x2_sum, x2_ready, x2_hi, x2_lo = sem("x2_sum"), sem("x2_ready"), sem("x2_hi"), sem("x2_lo")
        shift_ready, exp_ready, table_ready = sem("shift_ready"), sem("exp_ready"), sem("table_ready")
        sh_hi_ready, sh_lo_ready = sem("sh_hi_ready"), sem("sh_lo_ready")
        gate_ready, up_ready = sem("gate_ready"), sem("up_ready")
        act_done, prod_done = sem("act_done"), sem("prod_done")
        h_hi_done, h_lo_done = sem("h_hi_done"), sem("h_lo_done")
        down_done, acc_read = sem("down_done"), sem("acc_read")
        gu_hi_done, gu_lo_done = sem("gu_hi_done"), sem("gu_lo_done")
        wd_hi_done, wd_lo_done = sem("wd_hi_done"), sem("wd_lo_done")
        x3_hi, x3_lo = sem("x3_hi"), sem("x3_lo")

        block = ctx.enter_context(nc.Block())

        def rows(ap, b):
            return ap.unsqueeze(1).to_broadcast([P, b, ap.shape[-1]])

        @block.sync
        def _(sp):
            sp.dma_start(cond_sb[:, :, :], cond.unsqueeze(0).to_broadcast([P, B, E])).then_inc(d_small, DMA)
            sp.dma_start(const_sb[:, :], consts).then_inc(d_small, DMA)
            sp.dma_start(vec_sb[:, :], vecs).then_inc(d_small, DMA)
            sp.dma_start(w_l0_sb[:, :, :], w_l0).then_inc(d_lin, DMA)
            sp.dma_start(lin_sb[:, :, :], lin).then_inc(d_lin, DMA)
            sp.dma_start(x_in[:, :], xT).then_inc(d_x, DMA)
            sp.dma_start(w_all[:, SHARED_AT:], slabs[:, SHARED_AT:]).then_inc(d_shared, DMA)
            for e in range(E):
                at = slice(e * HALVES * SLAB, (e + 1) * HALVES * SLAB)
                sp.dma_start(w_all[:, at], slabs[:, at]).then_inc(d_experts, DMA)
            for e in range(0, E, 2):
                at = slice((SLABS_EXPERTS + e) * SLAB, (SLABS_EXPERTS + e + 2) * SLAB)
                sp.dma_start(w_all[:, at], slabs[:, at]).then_inc(d_l3, DMA)
            for b in range(B):
                sp.wait_ge(acc_read, PAIRS + B + b + 1)
                sp.dma_start(outT[:, b * S:(b + 1) * S], x_in[:, b * S:(b + 1) * S]).then_inc(d_out, DMA)
            sp.wait_ge(d_out, B * DMA)

        @block.tensor
        def _(pe):
            def mm(out, lhsT, rhs, start, stop):
                return nc.tensor.matmul(out, lhsT, rhs, start=start, stop=stop)

            def split_product(out, a_hi, a_lo, b_hi, b_lo, start=True, stop=True):
                mm(out, a_hi, b_hi, start, False)
                mm(out, a_lo, b_hi, False, False)
                return mm(out, a_hi, b_lo, False, stop)

            pe.wait_ge(y_ready, 1)
            pe.wait_ge(d_lin, 2 * DMA)
            for k in range(TBLK):
                at = (k % 4) * P
                last = mm(spare[k // 4][:, at:at + P], w_l0_sb[:, k, :],
                          y_diag[:].rearrange("p b t -> p (b t)"), True, True)
                if k % 4 == 3:
                    last.then_inc(w0_sum, 1)
            pe.wait_ge(bw_ready, 1)
            for k in range(2):
                mm(gate_ps[k][:], lora_a, lora_bw[:, 4 * k:4 * k + 4, :].rearrange("p b o -> p (b o)"),
                   True, True).then_inc(lora_sum, 1)
            for k in range(2):
                pe.wait_ge(w0_ready, 2)
                pe.wait_ge(r1_ready, k + 1)
                for b in range(4 * k, 4 * k + 4):
                    at = (b % 4) * P
                    last = mm(up_ps[k][:, at:at + P], w0_b[:, b, :], r1_b[:, b, :], True, True)
                last.then_inc(m_sum, 1)
            for b in range(B):
                last = mm(acc_ps[1][:, b:b + 1], r1_b[:, b, :], bias_l0, True, True)
            last.then_inc(c_sum, 1)
            x2_banks = [acc_ps[0], spare[0], spare[1], acc_ps[0]]
            pe.wait_ge(d_x, DMA)
            for p in range(PAIRS):
                pe.wait_ge(m_ready, p // 2 + 1)
                if p == 3:
                    pe.wait_ge(x2_ready, 1)
                for k in range(2):
                    b = 2 * p + k
                    last = mm(x2_banks[p][:, k * S:(k + 1) * S], m_b[:, b, :],
                              x_in[:, b * S:(b + 1) * S], True, True)
                last.then_inc(x2_sum, 1)

            def banks_free(u, first_use):
                if not first_use:
                    pe.wait_ge(act_done, u - 1)
                    pe.wait_ge(prod_done, u - 1)

            def shared_up(p, c, first_use=False):
                u = 4 * p + c
                banks_free(u, first_use)
                at = (c // 2) * SLAB + (c % 2) * P
                tok = bass.ds(p * PAIR, PAIR)
                for out, off, done in ((gate_ps[c % 2], 0, gate_ready), (up_ps[c % 2], 256, up_ready)):
                    w = slice(at + off, at + off + P)
                    split_product(out[:], sh_hi[:, w], sh_lo[:, w], x_hi[:, tok], x_lo[:, tok]).then_inc(done, 1)

            def hidden_split(u):
                pe.wait_ge(h_hi_done, u + 1)
                pe.wait_ge(h_lo_done, u + 1)

            def shared_down(p, c, first_use=False):
                u = 4 * p + c
                hidden_split(u)
                if c == 0 and not first_use:
                    pe.wait_ge(acc_read, p)
                at = (c // 2) * SLAB + SLAB_GU + (c % 2) * P
                w = slice(at, at + P)
                split_product(acc_ps[0][:], sh_hi[:, w], sh_lo[:, w], h_hi[:, c % 2, :], h_lo[:, c % 2, :],
                              c == 0, c == 3).then_inc(down_done, 1)

            def slab_up(u, q, slot, b):
                banks_free(u, False)
                pe.wait_ge(gu_hi_done, q + 1)
                pe.wait_ge(gu_lo_done, q + 1)
                tok = bass.ds(b * S, S)
                for out, off, done in ((gate_ps[slot % 2], 0, gate_ready), (up_ps[slot % 2], 256, up_ready)):
                    for c in range(2):
                        w = slice(off + c * P, off + (c + 1) * P)
                        last = split_product(out[:, c * S:(c + 1) * S], w_hi[:, slot, w], w_lo[:, slot, w],
                                             x_hi[:, tok], x_lo[:, tok])
                    last.then_inc(done, 1)

            def slab_down(u, q, slot, acc, start, stop):
                hidden_split(u)
                pe.wait_ge(wd_hi_done, q + 1)
                pe.wait_ge(wd_lo_done, q + 1)
                for c in range(2):
                    w = slice(SLAB_GU + c * P, SLAB_GU + (c + 1) * P)
                    h = slice(c * S, (c + 1) * S)
                    last = split_product(acc[:, 0:S], w_hi[:, slot, w], w_lo[:, slot, w],
                                         h_hi[:, slot % 2, h], h_lo[:, slot % 2, h],
                                         start and c == 0, stop and c == 1)
                last.then_inc(down_done, 1)

            def routed_down(b, j):
                if j == 0:
                    pe.wait_ge(acc_read, PAIRS + b)
                slab_down(R0 + 4 * b + j, 4 * b + j, j, acc_ps[0], j == 0, j == 3)

            pe.wait_ge(sh_hi_ready, HALVES)
            pe.wait_ge(sh_lo_ready, HALVES)
            pe.wait_ge(x2_hi, PAIRS)
            pe.wait_ge(x2_lo, PAIRS)
            for c in range(4):
                shared_up(0, c, first_use=c < 2)
                if c >= 2:
                    shared_down(0, c - 2, first_use=True)
            with pe.Fori(1, PAIRS) as p:
                for c in range(4):
                    shared_up(p, c)
                    shared_down(p if c >= 2 else p - 1, (c + 2) % 4)

            for j in range(4):
                slab_up(R0 + j, j, j, 0)
                if j < 2:
                    shared_down(PAIRS - 1, j + 2)
                else:
                    routed_down(0, j - 2)
            with pe.Fori(1, B) as b:
                for j in range(4):
                    slab_up(R0 + 4 * b + j, 4 * b + j, j, b)
                    routed_down(b if j >= 2 else b - 1, (j + 2) % 4)

            def l3_down(t):
                pe.wait_ge(acc_read, PAIRS + B + t - 1 if t else PAIRS + B)
                slab_down(T0 + t, UNITS_ROUTED + t, t % 4, acc_ps[t % 2], True, True)

            for t in range(B):
                pe.wait_ge(x3_hi, t + 1)
                pe.wait_ge(x3_lo, t + 1)
                slab_up(T0 + t, UNITS_ROUTED + t, t % 4, t)
                if t < 2:
                    routed_down(B - 1, t + 2)
                else:
                    l3_down(t - 2)
            l3_down(B - 2)
            l3_down(B - 1)

        @block.scalar
        def _(act):
            act.wait_ge(shift_ready, 1)
            nc.scalar.activation(expd[:], shifted[:], ACT.Exp).then_inc(exp_ready, 1)
            act.wait_ge(d_shared, DMA)
            for k in range(HALVES):
                at = slice(k * SLAB, (k + 1) * SLAB)
                nc.scalar.activation(sh_hi[:, at], w_all[:, SHARED_AT + k * SLAB:SHARED_AT + (k + 1) * SLAB],
                                     ACT.Copy).then_inc(sh_hi_ready, 1)
            for p in range(PAIRS):
                act.wait_ge(x2_ready, p + 1)
                at = slice(p * PAIR, (p + 1) * PAIR)
                nc.scalar.activation(x_hi[:, at], x_res[:, at], ACT.Copy).then_inc(x2_hi, 1)

            def gelu(u, k):
                act.wait_ge(gate_ready, u + 1)
                if not (isinstance(u, int) and u < 2):
                    act.wait_ge(prod_done, u - 1)
                nc.scalar.activation(h_act[:, k, :], gate_ps[k][:], ACT.Gelu_apprx_tanh).then_inc(act_done, 1)

            def round_h(u, k):
                act.wait_ge(prod_done, u + 1)
                if not (isinstance(u, int) and u < 2):
                    act.wait_ge(down_done, u - 1)
                nc.scalar.activation(h_hi[:, k, :], h_full[:, k, :], ACT.Copy).then_inc(h_hi_done, 1)

            def round_gate_up(q):
                slot = q % 4 if isinstance(q, int) else q[1]
                q = q if isinstance(q, int) else q[0]
                at = act.value_load(slab_at[0:1, bass.ds(q, 1)], min_val=0, max_val=SHARED_AT - SLAB)
                if not (isinstance(q, int) and q < 4):
                    act.wait_ge(up_ready, q + R0 - 3)
                nc.scalar.activation(w_hi[:, slot, 0:SLAB_GU], w_all[:, bass.ds(at, SLAB_GU)],
                                     ACT.Copy).then_inc(gu_hi_done, 1)

            def round_down(q):
                slot = q % 4 if isinstance(q, int) else q[1]
                q = q if isinstance(q, int) else q[0]
                at = act.value_load(slab_at[0:1, bass.ds(q, 1)], min_val=0, max_val=SHARED_AT - SLAB)
                if not (isinstance(q, int) and q < 4):
                    act.wait_ge(down_done, q + R0 - 3)
                nc.scalar.activation(w_hi[:, slot, SLAB_GU:], w_all[:, bass.ds(at + SLAB_GU, SLAB - SLAB_GU)],
                                     ACT.Copy).then_inc(wd_hi_done, 1)

            def round_x3(b):
                act.wait_ge(acc_read, PAIRS + b + 1)
                at = bass.ds(b * S, S)
                nc.scalar.activation(x_hi[:, at], x_res[:, at], ACT.Copy).then_inc(x3_hi, 1)

            gelu(0, 0)
            for c in range(1, 4):
                round_h(c - 1, (c - 1) % 2)
                gelu(c, c % 2)
            with act.Fori(1, PAIRS - 1) as p:
                for c in range(4):
                    round_h(4 * p + c - 1, (c - 1) % 2)
                    gelu(4 * p + c, c % 2)
            act.wait_ge(table_ready, 1)
            act.wait_ge(d_experts, E * DMA)
            for c in range(4):
                u = 4 * (PAIRS - 1) + c
                round_h(u - 1, (u - 1) % 2)
                gelu(u, u % 2)
                if c >= 1:
                    round_gate_up(c - 1)
                if c == 3:
                    round_down(0)

            def routed_batch(b, static):
                for j in range(4):
                    u = R0 + 4 * b + j
                    round_h(u - 1, (j - 1) % 2)
                    gelu(u, j % 2)
                    round_gate_up(4 * b + j + 3 if static else (4 * b + j + 3, (j + 3) % 4))
                    round_down(4 * b + j + 1 if static else (4 * b + j + 1, (j + 1) % 4))
                    if j == 2 and not static:
                        round_x3(b - 1)

            routed_batch(0, True)
            act.wait_ge(d_l3, E // 2 * DMA)
            with act.Fori(1, B) as b:
                routed_batch(b, False)
            for t in range(B):
                u = T0 + t
                round_h(u - 1, (u - 1) % 2)
                act.wait_ge(gate_ready, u + 1)
                act.wait_ge(prod_done, u - 1)
                for c in range(2):
                    last = nc.scalar.activation(h_act[:, t % 2, c * S:(c + 1) * S],
                                                gate_ps[t % 2][:, c * S:(c + 1) * S], ACT.Silu,
                                                bias=bias_b[:, c, t:t + 1])
                last.then_inc(act_done, 1)
                if UNITS_ROUTED + t + 3 < PREPS:
                    round_gate_up(UNITS_ROUTED + t + 3)
                if UNITS_ROUTED + t + 1 < PREPS:
                    round_down(UNITS_ROUTED + t + 1)
                if t == 2:
                    round_x3(B - 1)
            round_h(T0 + B - 1, (B - 1) % 2)

        @block.vector
        def _(dve):
            V = nc.vector
            steps = [0]

            def then(ins):
                steps[0] += 1
                ins.then_inc(dve_step, 1)
                dve.wait_ge(dve_step, steps[0])

            def over_e(ap):
                return ap.unsqueeze(2).to_broadcast([P, B, E])

            dve.wait_ge(d_small, 3 * DMA)
            then(V.tensor_tensor(cond_blk[:], cond_sb[:], rows(block_of, B), ALU.mult))
            then(V.tensor_reduce(cond_row[:], cond_blk[:], AX_X, ALU.add))
            V.tensor_tensor(y_diag[:], cond_row[:].unsqueeze(2).to_broadcast([P, B, RANK]),
                            rows(delta, B), ALU.mult).then_inc(y_ready, 1)
            then(V.tensor_reduce(top1[:], cond_sb[:], AX_X, ALU.max))
            V.tensor_tensor(shifted[:], cond_sb[:], over_e(top1[:]), ALU.subtract).then_inc(shift_ready, 1)
            dve.wait_ge(d_lin, 2 * DMA)
            V.scalar_tensor_tensor(lora_bw[:], rows(lora_bT, B), LORA_SCALE,
                                   cond_row[:].unsqueeze(2).to_broadcast([P, B, P]),
                                   ALU.mult, ALU.mult).then_inc(bw_ready, 1)
            then(V.tensor_tensor(base_i[:], ident, w_baseT, ALU.add))
            for k in range(2):
                dve.wait_ge(w0_sum, k + 1)
                kk = slice(4 * k, 4 * k + 4)
                V.tensor_tensor(
                    w0_b[:].rearrange("o b (k t) -> o k b t", t=RANK)[:, kk],
                    spare[k][:].rearrange("o (k b t) -> o k b t", k=4, t=RANK),
                    mask.rearrange("o (k t) -> o k t", t=RANK)[:, kk].unsqueeze(2).to_broadcast([P, 4, B, RANK]),
                    ALU.mult).then_inc(w0_ready, 1)
            for k in range(2):
                dve.wait_ge(lora_sum, k + 1)
                V.tensor_tensor(r1_b[:, 4 * k:4 * k + 4, :], gate_ps[k][:].rearrange("c (b o) -> c b o", b=4),
                                rows(base_i[:], 4), ALU.add).then_inc(r1_ready, 1)
            for k in range(2):
                dve.wait_ge(m_sum, k + 1)
                dve.wait_ge(r1_ready, k + 1)
                V.tensor_tensor(m_b[:, 4 * k:4 * k + 4, :], up_ps[k][:].rearrange("c (b o) -> c b o", b=4),
                                r1_b[:, 4 * k:4 * k + 4, :], ALU.add).then_inc(m_ready, 1)
            dve.wait_ge(c_sum, 1)
            then(V.tensor_scalar(c_b[:], acc_ps[1][:, 0:B], bias_l1, None, ALU.add))
            x2_banks = [acc_ps[0], spare[0], spare[1], acc_ps[0]]

            def lo_x2(p):
                dve.wait_ge(x2_hi, p + 1)
                at = slice(p * PAIR, (p + 1) * PAIR)
                V.tensor_tensor(x_lo[:, at], x_res[:, at], x_hi[:, at].bitcast(F32),
                                ALU.subtract).then_inc(x2_lo, 1)

            for p in range(PAIRS):
                dve.wait_ge(x2_sum, p + 1)
                V.tensor_tensor(x_res[:, p * PAIR:(p + 1) * PAIR].rearrange("o (b s) -> o b s", b=2),
                                x2_banks[p][:].rearrange("o (b s) -> o b s", b=2),
                                c_b[:, 2 * p:2 * p + 2].unsqueeze(2).to_broadcast([P, 2, S]),
                                ALU.add).then_inc(x2_ready, 1)
                if p:
                    lo_x2(p - 1)
            lo_x2(PAIRS - 1)
            for k in range(HALVES):
                at = slice(k * SLAB, (k + 1) * SLAB)
                dve.wait_ge(sh_hi_ready, k + 1)
                dve.wait_ge(d_shared, DMA)
                V.tensor_tensor(sh_lo[:, at], w_all[:, SHARED_AT + k * SLAB:SHARED_AT + (k + 1) * SLAB],
                                sh_hi[:, at].bitcast(F32), ALU.subtract).then_inc(sh_lo_ready, 1)

            def routing():
                then(V.tensor_tensor(hit[:, 0], cond_sb[:], over_e(top1[:]), ALU.is_equal))
                then(V.tensor_tensor(key[:], hit[:, 0], rows(rank_e, B), ALU.mult))
                then(V.tensor_reduce(first[:, 0], key[:], AX_X, ALU.max))
                then(V.tensor_tensor(one_hot[:, 0], rows(rank_e, B), over_e(first[:, 0]), ALU.is_equal))
                then(V.scalar_tensor_tensor(rest[:], one_hot[:, 0], -3.0e38, cond_sb[:], ALU.mult, ALU.add))
                then(V.tensor_reduce(top2[:], rest[:], AX_X, ALU.max))
                then(V.tensor_tensor(hit[:, 1], rest[:], over_e(top2[:]), ALU.is_equal))
                then(V.tensor_tensor(key[:], hit[:, 1], rows(rank_e, B), ALU.mult))
                then(V.tensor_reduce(first[:, 1], key[:], AX_X, ALU.max))
                then(V.tensor_tensor(one_hot[:, 1], rows(rank_e, B), over_e(first[:, 1]), ALU.is_equal))
                dve.wait_ge(exp_ready, 1)
                then(V.tensor_reduce(exp_sum[:], expd[:], AX_X, ALU.add))
                then(V.reciprocal(exp_sum[:], exp_sum[:]))
                then(V.tensor_tensor(probs[:], expd[:], over_e(exp_sum[:]), ALU.mult))
                for k in range(2):
                    then(V.tensor_tensor(picked[:, k], probs[:], one_hot[:, k], ALU.mult))
                then(V.tensor_reduce(w_pick[:], picked[:], AX_X, ALU.add))
                then(V.tensor_tensor(w_sum[:], w_pick[:, 0], w_pick[:, 1], ALU.add))
                then(V.reciprocal(w_sum[:], w_sum[:]))
                then(V.tensor_tensor(w_norm[:], w_pick[:], rows(w_sum[:], 2), ALU.mult))
                then(V.tensor_scalar(w_part[:], w_norm[:], 1.0 - MOE_LAYER_SCALE, None, ALU.mult))
                then(V.scalar_tensor_tensor(w_route[:].rearrange("p (b k) -> p k b", k=2), w_norm[:],
                                            MOE_LAYER_SCALE, w_part[:], ALU.mult, ALU.add))
                table = slab_at[0:1, 0:UNITS_ROUTED].rearrange("p (b k h) -> p k b h", k=2, h=HALVES)
                for k in range(2):
                    for h in range(HALVES):
                        V.tensor_scalar(table[:, k, :, h], first[0:1, k], -float(HALVES * SLAB),
                                        float((E * HALVES + h) * SLAB), ALU.mult, ALU.add)
                V.tensor_scalar(slab_at[0:1, UNITS_ROUTED:], first[0:1, 0], -float(SLAB),
                                float((SLABS_EXPERTS + E) * SLAB), ALU.mult, ALU.add).then_inc(table_ready, 1)
                for k in range(5):
                    last = V.tensor_tensor(bias_prod[:, k], rows(bias_l3[:, k], B), one_hot[:, 0], ALU.mult)
                then(last)
                then(V.tensor_reduce(bias_b[:], bias_prod[:], AX_X, ALU.add))

            def lo_h(u, k):
                dve.wait_ge(h_hi_done, u + 1)
                if not (isinstance(u, int) and u < 2):
                    dve.wait_ge(down_done, u - 1)
                V.tensor_tensor(h_lo[:, k, :], h_full[:, k, :], h_hi[:, k, :].bitcast(F32),
                                ALU.subtract).then_inc(h_lo_done, 1)

            def product(u, k, weight=None):
                dve.wait_ge(act_done, u + 1)
                dve.wait_ge(up_ready, u + 1)
                if weight is None:
                    ins = V.tensor_tensor(h_full[:, k, :], h_act[:, k, :], up_ps[k][:], ALU.mult)
                else:
                    ins = V.scalar_tensor_tensor(h_full[:, k, :], h_act[:, k, :], weight, up_ps[k][:],
                                                 ALU.mult, ALU.mult)
                ins.then_inc(prod_done, 1)

            def add_acc(at, n, down):
                dve.wait_ge(down_done, down)
                V.tensor_tensor(x_res[:, bass.ds(at, n)], acc_ps[0][:, 0:n], x_res[:, bass.ds(at, n)],
                                ALU.add).then_inc(acc_read, 1)

            def lo_gate_up(q, slot):
                at = dve.value_load(slab_at[0:1, bass.ds(q, 1)], min_val=0, max_val=SHARED_AT - SLAB)
                dve.wait_ge(gu_hi_done, q + 1)
                V.tensor_tensor(w_lo[:, slot, 0:SLAB_GU], w_all[:, bass.ds(at, SLAB_GU)],
                                w_hi[:, slot, 0:SLAB_GU].bitcast(F32), ALU.subtract).then_inc(gu_lo_done, 1)

            def lo_down(q, slot):
                at = dve.value_load(slab_at[0:1, bass.ds(q, 1)], min_val=0, max_val=SHARED_AT - SLAB)
                dve.wait_ge(wd_hi_done, q + 1)
                V.tensor_tensor(w_lo[:, slot, SLAB_GU:], w_all[:, bass.ds(at + SLAB_GU, SLAB - SLAB_GU)],
                                w_hi[:, slot, SLAB_GU:].bitcast(F32), ALU.subtract).then_inc(wd_lo_done, 1)

            def lo_x3(b):
                dve.wait_ge(x3_hi, b + 1)
                at = bass.ds(b * S, S)
                V.tensor_tensor(x_lo[:, at], x_res[:, at], x_hi[:, at].bitcast(F32),
                                ALU.subtract).then_inc(x3_lo, 1)

            product(0, 0)
            for c in range(1, 4):
                lo_h(c - 1, (c - 1) % 2)
                product(c, c % 2)
            routing()

            def shared_pair(p, last):
                for c in range(4):
                    u = 4 * p + c
                    lo_h(u - 1, (c - 1) % 2)
                    if c == 1:
                        add_acc((p - 1) * PAIR, PAIR, 4 * p)
                    product(u, c % 2)
                    if last and c >= 1:
                        lo_gate_up(c - 1, c - 1)
                    if last and c == 3:
                        lo_down(0, 0)

            with dve.Fori(1, PAIRS - 1) as p:
                shared_pair(p, False)
            dve.wait_ge(table_ready, 1)
            dve.wait_ge(d_experts, E * DMA)
            shared_pair(PAIRS - 1, True)

            def routed_batch(b, start):
                for j in range(4):
                    u = R0 + 4 * b + j
                    lo_h(u - 1, (j - 1) % 2)
                    if j == 1:
                        if start:
                            add_acc((PAIRS - 1) * PAIR, PAIR, R0)
                        else:
                            add_acc((b - 1) * S, S, R0 + 4 * b)
                    product(u, j % 2, w_route[:, bass.ds(2 * b + j // 2, 1)])
                    lo_gate_up(4 * b + j + 3, (j + 3) % 4)
                    lo_down(4 * b + j + 1, (j + 1) % 4)
                    if j == 3 and not start:
                        lo_x3(b - 1)

            routed_batch(0, True)
            dve.wait_ge(d_l3, E // 2 * DMA)
            with dve.Fori(1, B) as b:
                routed_batch(b, False)

            def finish(t):
                dve.wait_ge(down_done, T0 + t + 1)
                at = slice(t * S, (t + 1) * S)
                V.scalar_tensor_tensor(x_in[:, at], acc_ps[t % 2][:, 0:S], bias_b[:, 4, t:t + 1], x_res[:, at],
                                       ALU.add, ALU.add).then_inc(acc_read, 1)

            for t in range(B):
                u = T0 + t
                lo_h(u - 1, (u - 1) % 2)
                if t == 1:
                    add_acc((B - 1) * S, S, T0)
                if t >= 2:
                    finish(t - 2)
                dve.wait_ge(act_done, u + 1)
                dve.wait_ge(up_ready, u + 1)
                for c in range(2):
                    at = slice(c * S, (c + 1) * S)
                    last = V.scalar_tensor_tensor(h_full[:, t % 2, at], up_ps[t % 2][:, at],
                                                  bias_b[:, 2 + c, t:t + 1], h_act[:, t % 2, at],
                                                  ALU.add, ALU.mult)
                last.then_inc(prod_done, 1)
                if UNITS_ROUTED + t + 3 < PREPS:
                    lo_gate_up(UNITS_ROUTED + t + 3, (t + 3) % 4)
                if UNITS_ROUTED + t + 1 < PREPS:
                    lo_down(UNITS_ROUTED + t + 1, (t + 1) % 4)
                if t == 3:
                    lo_x3(B - 1)
            lo_h(T0 + B - 1, (B - 1) % 2)
            finish(B - 2)
            finish(B - 1)


def constants():
    p = np.arange(P)
    c = np.zeros((P, C_COLS), np.float32)
    c[:, C_BLOCK:C_BLOCK + E] = p[:, None] // RANK == np.arange(E)
    c[:, C_DELTA:C_DELTA + RANK] = p[:, None] % RANK == np.arange(RANK)
    c[:, C_RANK:C_RANK + E] = E - np.arange(E)
    c[:, C_IDENT:] = np.eye(P)
    return c


def kernel(x, cond_8, L0_cond_weight, L0_cond_mask, L0_cond_bias, L1_cond_W_base, L1_cond_b_base,
           L1_cond_As, L1_cond_Bs, L2_cond_skill_gate, L2_cond_skill_up, L2_cond_skill_down,
           L2_cond_shared_gate, L2_cond_shared_up, L2_cond_shared_down, L3_cond_W_up, L3_cond_b_up,
           L3_cond_W_gate, L3_cond_b_gate, L3_cond_W_down, L3_cond_b_down):
    import concourse.bacc as bacc
    from concourse.bass_utils import run_bass_kernel_spmd

    a = np.asarray
    cat = np.concatenate

    def moe_slabs(gate, up, down):
        n = gate.shape[0]
        cols = [w.reshape(n, D, HALVES, 256).transpose(1, 0, 2, 3) for w in (gate, up)]
        rows = down.reshape(n, HALVES, 2, P, D).transpose(3, 0, 1, 2, 4).reshape(P, n, HALVES, 2 * D)
        return cat([*cols, rows], axis=3).reshape(P, n * HALVES * SLAB)

    up3, gate3 = (a(w).transpose(2, 0, 1) for w in (L3_cond_W_up, L3_cond_W_gate))
    down3 = a(L3_cond_W_down).transpose(2, 0, 1).reshape(2, P, E, D).transpose(1, 2, 0, 3).reshape(P, E, 2 * D)
    slabs = cat([
        moe_slabs(a(L2_cond_skill_gate), a(L2_cond_skill_up), a(L2_cond_skill_down)),
        cat([up3, gate3, down3], axis=2).reshape(P, E * SLAB),
        moe_slabs(a(L2_cond_shared_gate)[None], a(L2_cond_shared_up)[None], a(L2_cond_shared_down)[None]),
    ], axis=1)
    w_l0 = a(L0_cond_weight).reshape(E, D, TBLK, RANK).transpose(0, 3, 2, 1).reshape(P, TBLK, D)
    lin = np.stack([a(L0_cond_mask), a(L1_cond_As).reshape(P, D),
                    a(L1_cond_Bs).transpose(0, 2, 1).reshape(P, D), a(L1_cond_W_base).T], axis=1)
    chunks = [a(v).reshape(E, 2, P).transpose(2, 1, 0).reshape(P, 2 * E) for v in (L3_cond_b_up, L3_cond_b_gate)]
    vecs = cat([a(L0_cond_bias)[:, None], a(L1_cond_b_base)[:, None], *chunks, a(L3_cond_b_down).T], axis=1)
    data = {
        "xT": a(x).transpose(2, 0, 1).reshape(P, TOKENS), "cond": a(cond_8), "consts": constants(),
        "w_l0": w_l0, "lin": lin, "vecs": vecs, "slabs": slabs,
    }
    data = {k: np.ascontiguousarray(v) for k, v in data.items()}

    nc = bacc.Bacc("TRN2", target_bir_lowering=False, num_devices=1)
    args = {k: nc.dram_tensor(k, v.shape, F32, kind="ExternalInput").ap() for k, v in data.items()}
    outT = nc.dram_tensor("outT", (P, TOKENS), F32, kind="ExternalOutput").ap()
    build(nc, outT=outT, **args)
    r = run_bass_kernel_spmd(nc, [data], core_ids=[0])
    got = r.results[0]["outT"]
    return np.ascontiguousarray(got.reshape(P, B, S).transpose(1, 2, 0))
```

```python
from contextlib import ExitStack

import numpy as np

import concourse.bass as bass
from concourse import mybir

F32 = mybir.dt.float32
F32R = mybir.dt.float32r
I32 = mybir.dt.int32
ALU = mybir.AluOpType
ACT = mybir.ActivationFunctionType
AX_X = mybir.AxisListType.X

P = 128
B, S, D = 8, 256, 128
E = 8
RANK = 16
LORA_SCALE = 32.0 / RANK
I_MOE = 512
H_L3 = 256
TOKENS = B * S
PAIR = 2 * S
PAIRS = B // 2
SLAB = 3 * 256
SLAB_GU = 512
HALVES = I_MOE // 256
SLABS_EXPERTS = E * HALVES
SLABS_L3 = E
SHARED_AT = (SLABS_EXPERTS + SLABS_L3) * SLAB
SLABS = SLABS_EXPERTS + SLABS_L3 + HALVES
MOE_LAYER_SCALE = 1.0 / 12
TBLK = D // RANK

UNITS_SHARED = PAIRS * 4
UNITS_ROUTED = B * 4
PREPS = UNITS_ROUTED + B
R0 = UNITS_SHARED
T0 = UNITS_SHARED + UNITS_ROUTED
W_SLOTS = 4
H_SLOTS = 4
DOWN_LAG = 3
ACC_AT = 2
ACC_BIAS = 2
WARM_UP = 6
DMA = 16

C_BLOCK = 0
C_DELTA = C_BLOCK + E
C_RANK = C_DELTA + RANK
C_IDENT = C_RANK + E
C_COLS = C_IDENT + P


def build(nc, xT, cond, consts, w_l0, lin, vecs, slabs, outT):
    with ExitStack() as ctx:
        def sb(name, shape, dt=F32):
            return ctx.enter_context(nc.sbuf_tensor(name, shape, dt))

        def bank(name):
            return ctx.enter_context(nc.psum_tensor(name, [P, 512], F32))

        def sem(name):
            return ctx.enter_context(nc.semaphore(name))

        w_all = sb("w_all", [P, SLABS * SLAB])
        x_in = sb("x_in", [P, TOKENS])
        cond_sb = sb("cond_sb", [P, B, E])
        const_sb = sb("const_sb", [P, C_COLS])
        w_l0_sb = sb("w_l0_sb", [P, TBLK, P])
        lin_sb = sb("lin_sb", [P, 4, P])
        vec_sb = sb("vec_sb", [P, 2 + 5 * E])
        block_of = const_sb[:, C_BLOCK:C_BLOCK + E]
        delta = const_sb[:, C_DELTA:C_DELTA + RANK]
        rank_e = const_sb[:, C_RANK:C_RANK + E]
        ident = const_sb[:, C_IDENT:C_IDENT + P]
        mask, lora_a, lora_bT, w_baseT = (lin_sb[:, k, :] for k in range(4))
        bias_l0, bias_l1 = vec_sb[:, 0:1], vec_sb[:, 1:2]
        bias_l3 = vec_sb[:, 2:].rearrange("p (k e) -> p k e", e=E)

        cond_blk = sb("cond_blk", [P, B, E])
        cond_row = sb("cond_row", [P, B])
        cond_scaled = sb("cond_scaled", [P, B])
        y_diag = sb("y_diag", [P, B, RANK])
        lora_bw = sb("lora_bw", [P, B, P])
        base_i = sb("base_i", [P, P])
        w0_b = sb("w0_b", [P, B, P])
        r1_b = sb("r1_b", [P, B, P])
        m_b = sb("m_b", [P, B, P])
        c_b = sb("c_b", [P, B])
        x_res = sb("x_res", [P, TOKENS])
        x_hi = sb("x_hi", [P, TOKENS], F32R)
        x_lo = sb("x_lo", [P, TOKENS], F32R)

        top1 = sb("top1", [P, B])
        shifted = sb("shifted", [P, B, E])
        expd = sb("expd", [P, B, E])
        exp_sum = sb("exp_sum", [P, B])
        probs = sb("probs", [P, B, E])
        hit = sb("hit", [P, 2, B, E])
        key = sb("key", [P, B, E])
        first = sb("first", [P, 2, B])
        one_hot = sb("one_hot", [P, 2, B, E])
        rest = sb("rest", [P, B, E])
        top2 = sb("top2", [P, B])
        picked = sb("picked", [P, 2, B, E])
        w_pick = sb("w_pick", [P, 2, B])
        w_sum = sb("w_sum", [P, B])
        w_norm = sb("w_norm", [P, 2, B])
        w_part = sb("w_part", [P, 2, B])
        w_route = sb("w_route", [P, 2 * B])
        slab_at = sb("slab_at", [1, PREPS], I32)
        bias_prod = sb("bias_prod", [P, 5, B, E])
        bias_b = sb("bias_b", [P, 5, B])

        sh_hi = sb("sh_hi", [P, HALVES * SLAB], F32R)
        sh_lo = sb("sh_lo", [P, HALVES * SLAB], F32R)
        w_hi = sb("w_hi", [P, W_SLOTS, SLAB], F32R)
        w_lo = sb("w_lo", [P, W_SLOTS, SLAB], F32R)
        h_act = sb("h_act", [P, 2, 512])
        h_full = sb("h_full", [P, H_SLOTS, 512])
        h_hi = sb("h_hi", [P, H_SLOTS, 512], F32R)
        h_lo = sb("h_lo", [P, H_SLOTS, 512], F32R)
        zeros = sb("zeros", [P, S])

        gate_ps = [bank("gate0"), bank("gate1")]
        up_ps = [bank("up0"), bank("up1")]
        acc_ps = ctx.enter_context(nc.psum_tensor("acc", [P, 2 * 512], F32))
        spare = [bank("spare0"), bank("spare1")]
        m_banks = [gate_ps[0], up_ps[0], gate_ps[1], up_ps[1]]
        c_banks = [acc_ps[:, 0:512], acc_ps[:, 512:1024]]

        d_small, d_vecs, d_lin, d_w_l0, d_x, d_shared, d_experts, d_l3 = (
            sem(n) for n in ("d_small", "d_vecs", "d_lin", "d_w_l0", "d_x", "d_shared", "d_experts", "d_l3"))
        d_out = sem("d_out")
        dve_step, zeros_ready = sem("dve_step"), sem("zeros_ready")
        scaled_ready, bias_prod_ready = sem("scaled_ready"), sem("bias_prod_ready")
        y_ready, bw_ready = sem("y_ready"), sem("bw_ready")
        w0_sum, lora_sum = sem("w0_sum"), sem("lora_sum")
        w0_ready, r1_ready = sem("w0_ready"), sem("r1_ready")
        m_sum, m_ready = sem("m_sum"), sem("m_ready")
        c_sum = sem("c_sum")
        x2_sum, x2_ready, x2_hi, x2_lo = sem("x2_sum"), sem("x2_ready"), sem("x2_hi"), sem("x2_lo")
        shift_ready, exp_ready, table_ready = sem("shift_ready"), sem("exp_ready"), sem("table_ready")
        sh_hi_ready, sh_lo_ready = sem("sh_hi_ready"), sem("sh_lo_ready")
        gate_ready, up_ready = sem("gate_ready"), sem("up_ready")
        act_done, prod_done = sem("act_done"), sem("prod_done")
        h_hi_done, h_lo_done = sem("h_hi_done"), sem("h_lo_done")
        down_done = sem("down_done")
        acc_read = sem("acc_read")
        gu_hi_done, gu_lo_done = sem("gu_hi_done"), sem("gu_lo_done")
        wd_hi_done, wd_lo_done = sem("wd_hi_done"), sem("wd_lo_done")
        x3_hi, x3_lo = sem("x3_hi"), sem("x3_lo")

        block = ctx.enter_context(nc.Block())

        def acc(group, n):
            return acc_ps[:, bass.ds((group % 2) * 512, n)]

        def rows(ap, b):
            return ap.unsqueeze(1).to_broadcast([P, b, ap.shape[-1]])

        @block.sync
        def _(sp):
            sp.dma_start(cond_sb[:, :, :], cond.unsqueeze(0).to_broadcast([P, B, E])).then_inc(d_small, DMA)
            sp.dma_start(const_sb[:, :], consts).then_inc(d_small, DMA)
            sp.dma_start(lin_sb[:, :, :], lin).then_inc(d_lin, DMA)
            sp.dma_start(x_in[:, :], xT).then_inc(d_x, DMA)
            sp.dma_start(w_all[:, SHARED_AT:], slabs[:, SHARED_AT:]).then_inc(d_shared, DMA)
            for e in range(E):
                at = slice(e * HALVES * SLAB, (e + 1) * HALVES * SLAB)
                sp.dma_start(w_all[:, at], slabs[:, at]).then_inc(d_experts, DMA)
            for e in range(0, E, 2):
                at = slice((SLABS_EXPERTS + e) * SLAB, (SLABS_EXPERTS + e + 2) * SLAB)
                sp.dma_start(w_all[:, at], slabs[:, at]).then_inc(d_l3, DMA)
            for b in range(B):
                sp.wait_ge(acc_read, ACC_BIAS + PAIRS + B + b + 1)
                sp.dma_start(outT[:, b * S:(b + 1) * S], x_in[:, b * S:(b + 1) * S]).then_inc(d_out, DMA)
            sp.wait_ge(d_out, B * DMA)

        @block.tensor
        def _(pe):
            def mm(out, lhsT, rhs, start, stop):
                return nc.tensor.matmul(out, lhsT, rhs, start=start, stop=stop)

            def split_product(out, a_hi, a_lo, b_hi, b_lo, start=True, stop=True):
                mm(out, a_hi, b_hi, start, False)
                mm(out, a_hi, b_lo, False, False)
                return mm(out, a_lo, b_hi, False, stop)

            pe.wait_ge(zeros_ready, 1)
            for _ in range(WARM_UP):
                mm(acc_ps[:, 0:S], zeros[:, 0:P], zeros[:], True, True)
            pe.wait_ge(y_ready, 1)
            pe.wait_ge(d_w_l0, DMA)
            for k in range(2):
                for i in range(4):
                    last = mm(spare[k][:, i * P:(i + 1) * P], w_l0_sb[:, 4 * k + i, :],
                              y_diag[:].rearrange("p b t -> p (b t)"), True, True)
                last.then_inc(w0_sum, 1)
                pe.wait_ge(bw_ready, k + 1)
                mm(gate_ps[k][:], lora_a, lora_bw[:, 4 * k:4 * k + 4, :].rearrange("p b o -> p (b o)"),
                   True, True).then_inc(lora_sum, 1)
            pe.wait_ge(d_vecs, DMA)

            def bias_and_matrix(k):
                pe.wait_ge(r1_ready, k + 1)
                for b in range(4 * k, 4 * k + 4):
                    last = mm(c_banks[k][:, b % 4:b % 4 + 1], r1_b[:, b, :], bias_l0, True, True)
                last.then_inc(c_sum, 1)
                pe.wait_ge(w0_ready, 2)
                for b in range(4 * k, 4 * k + 4):
                    at = (b % 2) * P
                    last = mm(m_banks[b // 2][:, at:at + P], w0_b[:, b, :], r1_b[:, b, :], True, True)
                    if b % 2 == 1:
                        last.then_inc(m_sum, 1)

            bias_and_matrix(0)
            pe.wait_ge(d_x, DMA)

            def x2(p):
                pe.wait_ge(m_ready, p + 1)
                if p >= 2:
                    pe.wait_ge(x2_ready, p - 1)
                for k in range(2):
                    b = 2 * p + k
                    last = mm(spare[p % 2][:, k * S:(k + 1) * S], m_b[:, b, :],
                              x_in[:, b * S:(b + 1) * S], True, True)
                last.then_inc(x2_sum, 1)

            def banks_free(u, first_use):
                if not first_use:
                    pe.wait_ge(act_done, u - 1)
                    pe.wait_ge(prod_done, u - 1)

            def shared_up(p, c, first_use=False):
                u = 4 * p + c
                banks_free(u, first_use)
                at = (c // 2) * SLAB + (c % 2) * P
                tok = bass.ds(p * PAIR, PAIR)
                for out, off, done in ((gate_ps[c % 2], 0, gate_ready), (up_ps[c % 2], 256, up_ready)):
                    w = slice(at + off, at + off + P)
                    split_product(out[:], sh_hi[:, w], sh_lo[:, w], x_hi[:, tok], x_lo[:, tok]).then_inc(done, 1)

            def hidden_split(u):
                pe.wait_ge(h_hi_done, u + 1)
                pe.wait_ge(h_lo_done, u + 1)

            def acc_bank_free(group):
                pe.wait_ge(acc_read, group + 1)

            def shared_down(p, c):
                u = 4 * p + c
                hidden_split(u)
                if c == 0:
                    acc_bank_free(p)
                at = (c // 2) * SLAB + SLAB_GU + (c % 2) * P
                w = slice(at, at + P)
                split_product(acc(p, 512), sh_hi[:, w], sh_lo[:, w], h_hi[:, c, :], h_lo[:, c, :],
                              c == 0, c == 3).then_inc(down_done, 1)

            def slab_up(u, q, slot, b):
                banks_free(u, False)
                pe.wait_ge(gu_hi_done, q + 1)
                pe.wait_ge(gu_lo_done, q + 1)
                tok = bass.ds(b * S, S)
                for out, off, done in ((gate_ps[slot % 2], 0, gate_ready), (up_ps[slot % 2], 256, up_ready)):
                    for c in range(2):
                        w = slice(off + c * P, off + (c + 1) * P)
                        last = split_product(out[:, c * S:(c + 1) * S], w_hi[:, slot, w], w_lo[:, slot, w],
                                             x_hi[:, tok], x_lo[:, tok])
                    last.then_inc(done, 1)

            def slab_down(u, q, slot, group, start, stop):
                hidden_split(u)
                pe.wait_ge(wd_hi_done, q + 1)
                pe.wait_ge(wd_lo_done, q + 1)
                for c in range(2):
                    w = slice(SLAB_GU + c * P, SLAB_GU + (c + 1) * P)
                    h = slice(c * S, (c + 1) * S)
                    last = split_product(acc(group, S), w_hi[:, slot, w], w_lo[:, slot, w],
                                         h_hi[:, slot, h], h_lo[:, slot, h],
                                         start and c == 0, stop and c == 1)
                last.then_inc(down_done, 1)

            def routed_down(b, j):
                if j == 0:
                    acc_bank_free(PAIRS + b)
                slab_down(R0 + 4 * b + j, 4 * b + j, j, b, j == 0, j == 3)

            x2(0)
            bias_and_matrix(1)
            pe.wait_ge(x2_hi, 1)
            pe.wait_ge(x2_lo, 1)
            for c in range(4):
                pe.wait_ge(sh_hi_ready, c // 2 + 1)
                pe.wait_ge(sh_lo_ready, c // 2 + 1)
                if c < 2:
                    pe.wait_ge(m_ready, 2 * (c + 1))
                shared_up(0, c, first_use=c < 2)
                if c + 1 < PAIRS:
                    x2(c + 1)
                if c >= DOWN_LAG:
                    shared_down(0, c - DOWN_LAG)
            with pe.Fori(1, PAIRS) as p:
                pe.wait_ge(x2_hi, p + 1)
                pe.wait_ge(x2_lo, p + 1)
                for c in range(4):
                    shared_up(p, c)
                    shared_down(p if c >= DOWN_LAG else p - 1, (c - DOWN_LAG) % 4)

            for j in range(4):
                slab_up(R0 + j, j, j, 0)
                if j < DOWN_LAG:
                    shared_down(PAIRS - 1, 4 + j - DOWN_LAG)
                else:
                    routed_down(0, j - DOWN_LAG)
            with pe.Fori(1, B) as b:
                for j in range(4):
                    slab_up(R0 + 4 * b + j, 4 * b + j, j, b)
                    routed_down(b if j >= DOWN_LAG else b - 1, (j - DOWN_LAG) % 4)

            def l3_down(t):
                acc_bank_free(PAIRS + B + t)
                slab_down(T0 + t, UNITS_ROUTED + t, t % 4, t, True, True)

            for t in range(B):
                pe.wait_ge(x3_hi, t + 1)
                pe.wait_ge(x3_lo, t + 1)
                slab_up(T0 + t, UNITS_ROUTED + t, t % 4, t)
                if t < DOWN_LAG:
                    routed_down(B - 1, 4 + t - DOWN_LAG)
                else:
                    l3_down(t - DOWN_LAG)
            for t in range(B - DOWN_LAG, B):
                l3_down(t)

        @block.scalar
        def _(act):
            act.dma_start(w_l0_sb[:, :, :], w_l0).then_inc(d_w_l0, DMA)
            act.dma_start(vec_sb[:, :], vecs).then_inc(d_vecs, DMA)
            act.wait_ge(shift_ready, 1)
            nc.scalar.activation(expd[:], shifted[:], ACT.Exp).then_inc(exp_ready, 1)
            act.wait_ge(d_shared, DMA)
            for k in range(HALVES):
                at = slice(k * SLAB, (k + 1) * SLAB)
                nc.scalar.activation(sh_hi[:, at], w_all[:, SHARED_AT + k * SLAB:SHARED_AT + (k + 1) * SLAB],
                                     ACT.Copy).then_inc(sh_hi_ready, 1)
            def x2(p):
                act.wait_ge(x2_sum, p + 1)
                act.wait_ge(acc_read, p // 2 + 1)
                for b in (2 * p, 2 * p + 1):
                    last = nc.scalar.activation(x_res[:, b * S:(b + 1) * S],
                                                spare[p % 2][:, (b % 2) * S:(b % 2 + 1) * S],
                                                ACT.Identity, bias=c_b[:, b:b + 1])
                last.then_inc(x2_ready, 1)
                act.wait_ge(x2_ready, p + 1)
                at = slice(p * PAIR, (p + 1) * PAIR)
                nc.scalar.activation(x_hi[:, at], x_res[:, at], ACT.Copy).then_inc(x2_hi, 1)

            x2(0)

            def gelu(u, k):
                act.wait_ge(gate_ready, u + 1)
                if not (isinstance(u, int) and u < 2):
                    act.wait_ge(prod_done, u - 1)
                nc.scalar.activation(h_act[:, k, :], gate_ps[k][:], ACT.Gelu_apprx_tanh).then_inc(act_done, 1)

            def round_h(u, slot):
                act.wait_ge(prod_done, u + 1)
                if not (isinstance(u, int) and u < H_SLOTS):
                    act.wait_ge(down_done, u + 1 - H_SLOTS)
                nc.scalar.activation(h_hi[:, slot, :], h_full[:, slot, :], ACT.Copy).then_inc(h_hi_done, 1)

            def round_gate_up(q):
                slot = q % 4 if isinstance(q, int) else q[1]
                q = q if isinstance(q, int) else q[0]
                at = act.value_load(slab_at[0:1, bass.ds(q, 1)], min_val=0, max_val=SHARED_AT - SLAB)
                if not (isinstance(q, int) and q < 4):
                    act.wait_ge(up_ready, q + R0 - 3)
                nc.scalar.activation(w_hi[:, slot, 0:SLAB_GU], w_all[:, bass.ds(at, SLAB_GU)],
                                     ACT.Copy).then_inc(gu_hi_done, 1)

            def round_down(q):
                slot = q % 4 if isinstance(q, int) else q[1]
                q = q if isinstance(q, int) else q[0]
                at = act.value_load(slab_at[0:1, bass.ds(q, 1)], min_val=0, max_val=SHARED_AT - SLAB)
                if not (isinstance(q, int) and q < 4):
                    act.wait_ge(down_done, q + R0 - 3)
                nc.scalar.activation(w_hi[:, slot, SLAB_GU:], w_all[:, bass.ds(at + SLAB_GU, SLAB - SLAB_GU)],
                                     ACT.Copy).then_inc(wd_hi_done, 1)

            def round_x3(b):
                act.wait_ge(acc_read, ACC_BIAS + PAIRS + b + 1)
                at = bass.ds(b * S, S)
                nc.scalar.activation(x_hi[:, at], x_res[:, at], ACT.Copy).then_inc(x3_hi, 1)

            gelu(0, 0)
            for c in range(1, 4):
                x2(c)
                gelu(c, c % 2)
                round_h(c - 1, c - 1)
            with act.Fori(1, PAIRS - 1) as p:
                for c in range(4):
                    gelu(4 * p + c, c % 2)
                    round_h(4 * p + c - 1, (c - 1) % 4)
            act.wait_ge(table_ready, 1)
            act.wait_ge(d_experts, E * DMA)
            for c in range(4):
                u = 4 * (PAIRS - 1) + c
                gelu(u, u % 2)
                round_h(u - 1, (u - 1) % 4)
                if c >= 1:
                    round_gate_up(c - 1)
                if c == 3:
                    round_down(0)

            def routed_batch(b, static):
                for j in range(4):
                    u = R0 + 4 * b + j
                    gelu(u, j % 2)
                    round_h(u - 1, (j - 1) % 4)
                    round_gate_up(4 * b + j + 3 if static else (4 * b + j + 3, (j + 3) % 4))
                    round_down(4 * b + j + 1 if static else (4 * b + j + 1, (j + 1) % 4))
                    if j == 3 and not static:
                        round_x3(b - 1)

            routed_batch(0, True)
            act.wait_ge(d_l3, E // 2 * DMA)
            with act.Fori(1, B) as b:
                routed_batch(b, False)
            for t in range(B):
                u = T0 + t
                act.wait_ge(gate_ready, u + 1)
                act.wait_ge(prod_done, u - 1)
                for c in range(2):
                    last = nc.scalar.activation(h_act[:, t % 2, c * S:(c + 1) * S],
                                                gate_ps[t % 2][:, c * S:(c + 1) * S], ACT.Silu,
                                                bias=bias_b[:, c, t:t + 1])
                last.then_inc(act_done, 1)
                round_h(u - 1, (u - 1) % 4)
                if UNITS_ROUTED + t + 3 < PREPS:
                    round_gate_up(UNITS_ROUTED + t + 3)
                if UNITS_ROUTED + t + 1 < PREPS:
                    round_down(UNITS_ROUTED + t + 1)
                if t == 3:
                    round_x3(B - 1)
            round_h(T0 + B - 1, (B - 1) % 4)

        @block.gpsimd
        def _(pool):
            pool.wait_ge(scaled_ready, 1)
            pool.wait_ge(d_lin, DMA)
            for k in range(2):
                bb = slice(4 * k, 4 * k + 4)
                nc.gpsimd.tensor_tensor(lora_bw[:, bb], rows(lora_bT, 4),
                                        cond_scaled[:, bb].unsqueeze(2).to_broadcast([P, 4, P]),
                                        ALU.mult).then_inc(bw_ready, 1)
            pool.wait_ge(d_shared, DMA)
            for k in range(HALVES):
                at = slice(k * SLAB, (k + 1) * SLAB)
                pool.wait_ge(sh_hi_ready, k + 1)
                nc.gpsimd.tensor_tensor(sh_lo[:, at], w_all[:, SHARED_AT + k * SLAB:SHARED_AT + (k + 1) * SLAB],
                                        sh_hi[:, at].bitcast(F32), ALU.subtract).then_inc(sh_lo_ready, 1)
            for p in range(1, PAIRS):
                pool.wait_ge(x2_hi, p + 1)
                at = slice(p * PAIR, (p + 1) * PAIR)
                nc.gpsimd.tensor_tensor(x_lo[:, at], x_res[:, at], x_hi[:, at].bitcast(F32),
                                        ALU.subtract).then_inc(x2_lo, 1)

            pool.wait_ge(table_ready, 1)
            pool.wait_ge(d_vecs, DMA)
            for k in range(5):
                nc.gpsimd.tensor_tensor(bias_prod[:, k], rows(bias_l3[:, k], B), one_hot[:, 0],
                                        ALU.mult).then_inc(bias_prod_ready, 1)

            def lo_down(q, slot):
                at = pool.value_load(slab_at[0:1, bass.ds(q, 1)], min_val=0, max_val=SHARED_AT - SLAB)
                pool.wait_ge(wd_hi_done, q + 1)
                nc.gpsimd.tensor_tensor(w_lo[:, slot, SLAB_GU:], w_all[:, bass.ds(at + SLAB_GU, SLAB - SLAB_GU)],
                                        w_hi[:, slot, SLAB_GU:].bitcast(F32), ALU.subtract).then_inc(wd_lo_done, 1)

            def lo_x3(b):
                pool.wait_ge(x3_hi, b + 1)
                at = bass.ds(b * S, S)
                nc.gpsimd.tensor_tensor(x_lo[:, at], x_res[:, at], x_hi[:, at].bitcast(F32),
                                        ALU.subtract).then_inc(x3_lo, 1)

            pool.wait_ge(table_ready, 1)
            pool.wait_ge(d_experts, E * DMA)
            for q in range(5):
                lo_down(q, q % 4)
            pool.wait_ge(d_l3, E // 2 * DMA)
            with pool.Fori(1, B) as b:
                for j in range(4):
                    lo_down(4 * b + j + 1, (j + 1) % 4)
                    if j == 3:
                        lo_x3(b - 1)
            for q in range(UNITS_ROUTED + 1, PREPS):
                lo_down(q, q % 4)
                if q == UNITS_ROUTED + 4:
                    lo_x3(B - 1)

        @block.vector
        def _(dve):
            V = nc.vector
            steps = [0]

            def then(ins):
                steps[0] += 1
                ins.then_inc(dve_step, 1)
                dve.wait_ge(dve_step, steps[0])

            def over_e(ap):
                return ap.unsqueeze(2).to_broadcast([P, B, E])

            def choose():
                then(V.tensor_tensor(hit[:, 0], cond_sb[:], over_e(top1[:]), ALU.is_equal))
                then(V.tensor_tensor(key[:], hit[:, 0], rows(rank_e, B), ALU.mult))
                then(V.tensor_reduce(first[:, 0], key[:], AX_X, ALU.max))
                then(V.tensor_tensor(one_hot[:, 0], rows(rank_e, B), over_e(first[:, 0]), ALU.is_equal))

            def choose_second():
                then(V.scalar_tensor_tensor(rest[:], one_hot[:, 0], -3.0e38, cond_sb[:], ALU.mult, ALU.add))
                then(V.tensor_reduce(top2[:], rest[:], AX_X, ALU.max))
                then(V.tensor_tensor(hit[:, 1], rest[:], over_e(top2[:]), ALU.is_equal))
                then(V.tensor_tensor(key[:], hit[:, 1], rows(rank_e, B), ALU.mult))
                then(V.tensor_reduce(first[:, 1], key[:], AX_X, ALU.max))
                then(V.tensor_tensor(one_hot[:, 1], rows(rank_e, B), over_e(first[:, 1]), ALU.is_equal))

            def weigh():
                dve.wait_ge(exp_ready, 1)
                then(V.tensor_reduce(exp_sum[:], expd[:], AX_X, ALU.add))
                then(V.reciprocal(exp_sum[:], exp_sum[:]))
                then(V.tensor_tensor(probs[:], expd[:], over_e(exp_sum[:]), ALU.mult))
                then(V.tensor_tensor(picked[:].rearrange("p k b e -> p k (b e)"),
                                     one_hot[:].rearrange("p k b e -> p k (b e)"),
                                     rows(probs[:].rearrange("p b e -> p (b e)"), 2), ALU.mult))
                then(V.tensor_reduce(w_pick[:], picked[:], AX_X, ALU.add))

            def normalise():
                then(V.tensor_tensor(w_sum[:], w_pick[:, 0], w_pick[:, 1], ALU.add))
                then(V.reciprocal(w_sum[:], w_sum[:]))
                then(V.tensor_tensor(w_norm[:], w_pick[:], rows(w_sum[:], 2), ALU.mult))
                then(V.tensor_scalar(w_part[:], w_norm[:], 1.0 - MOE_LAYER_SCALE, None, ALU.mult))
                then(V.scalar_tensor_tensor(w_route[:].rearrange("p (b k) -> p k b", k=2), w_norm[:],
                                            MOE_LAYER_SCALE, w_part[:], ALU.mult, ALU.add))

            def tabulate():
                table = slab_at[0:1, 0:UNITS_ROUTED].rearrange("p (b k h) -> p k b h", k=2, h=HALVES)
                for k in range(2):
                    for h in range(HALVES):
                        V.tensor_scalar(table[:, k, :, h], first[0:1, k], -float(HALVES * SLAB),
                                        float((E * HALVES + h) * SLAB), ALU.mult, ALU.add)
                V.tensor_scalar(slab_at[0:1, UNITS_ROUTED:], first[0:1, 0], -float(SLAB),
                                float((SLABS_EXPERTS + E) * SLAB), ALU.mult, ALU.add).then_inc(table_ready, 1)

            def choose_biases():
                then(V.tensor_reduce(bias_b[:], bias_prod[:], AX_X, ALU.add))

            V.memset(zeros[:], 0.0).then_inc(zeros_ready, 1)
            dve.wait_ge(d_small, 2 * DMA)
            then(V.tensor_tensor(cond_blk[:], cond_sb[:], rows(block_of, B), ALU.mult))
            then(V.tensor_reduce(cond_row[:], cond_blk[:], AX_X, ALU.add))
            V.tensor_tensor(y_diag[:], cond_row[:].unsqueeze(2).to_broadcast([P, B, RANK]),
                            rows(delta, B), ALU.mult).then_inc(y_ready, 1)
            V.tensor_scalar(cond_scaled[:], cond_row[:], LORA_SCALE, None, ALU.mult).then_inc(scaled_ready, 1)
            then(V.tensor_reduce(top1[:], cond_sb[:], AX_X, ALU.max))
            V.tensor_tensor(shifted[:], cond_sb[:], over_e(top1[:]), ALU.subtract).then_inc(shift_ready, 1)
            choose()
            dve.wait_ge(d_lin, DMA)
            then(V.tensor_tensor(base_i[:], ident, w_baseT, ALU.add))
            for k in range(2):
                dve.wait_ge(w0_sum, k + 1)
                kk = slice(4 * k, 4 * k + 4)
                V.tensor_tensor(
                    w0_b[:].rearrange("o b (k t) -> o k b t", t=RANK)[:, kk],
                    spare[k][:].rearrange("o (k b t) -> o k b t", k=4, t=RANK),
                    mask.rearrange("o (k t) -> o k t", t=RANK)[:, kk].unsqueeze(2).to_broadcast([P, 4, B, RANK]),
                    ALU.mult).then_inc(w0_ready, 1)
                dve.wait_ge(lora_sum, k + 1)
                V.tensor_tensor(r1_b[:, 4 * k:4 * k + 4, :], gate_ps[k][:].rearrange("c (b o) -> c b o", b=4),
                                rows(base_i[:], 4), ALU.add).then_inc(r1_ready, 1)
            dve.wait_ge(r1_ready, 2)
            dve.wait_ge(d_vecs, DMA)
            for k in range(PAIRS):
                if k % 2 == 0:
                    dve.wait_ge(c_sum, k // 2 + 1)
                    V.tensor_scalar(c_b[:, 2 * k:2 * k + 4], c_banks[k // 2][:, 0:4], bias_l1, None,
                                    ALU.add).then_inc(acc_read, 1)
                dve.wait_ge(m_sum, k + 1)
                bb = slice(2 * k, 2 * k + 2)
                V.tensor_tensor(m_b[:, bb, :],
                                m_banks[k][:, 0:2 * P].rearrange("c (b o) -> c b o", b=2),
                                r1_b[:, bb, :], ALU.add).then_inc(m_ready, 1)
                if k == 1:
                    choose_second()
                if k == 2:
                    dve.wait_ge(x2_hi, 1)
                    V.tensor_tensor(x_lo[:, 0:PAIR], x_res[:, 0:PAIR], x_hi[:, 0:PAIR].bitcast(F32),
                                    ALU.subtract).then_inc(x2_lo, 1)
            tabulate()

            def lo_h(u, slot):
                dve.wait_ge(h_hi_done, u + 1)
                V.tensor_tensor(h_lo[:, slot, :], h_full[:, slot, :], h_hi[:, slot, :].bitcast(F32),
                                ALU.subtract).then_inc(h_lo_done, 1)

            def full_slot_free(u):
                if not (isinstance(u, int) and u < H_SLOTS):
                    dve.wait_ge(h_lo_done, u + 1 - H_SLOTS)

            def product(u, slot, weight=None):
                k = slot % 2
                full_slot_free(u)
                dve.wait_ge(act_done, u + 1)
                dve.wait_ge(up_ready, u + 1)
                if weight is None:
                    ins = V.tensor_tensor(h_full[:, slot, :], h_act[:, k, :], up_ps[k][:], ALU.mult)
                else:
                    ins = V.scalar_tensor_tensor(h_full[:, slot, :], h_act[:, k, :], weight, up_ps[k][:],
                                                 ALU.mult, ALU.mult)
                ins.then_inc(prod_done, 1)

            def add_acc(group, n, down):
                at = group * n
                dve.wait_ge(down_done, down)
                V.tensor_tensor(x_res[:, bass.ds(at, n)], acc(group, n), x_res[:, bass.ds(at, n)],
                                ALU.add).then_inc(acc_read, 1)

            def lo_gate_up(q, slot):
                at = dve.value_load(slab_at[0:1, bass.ds(q, 1)], min_val=0, max_val=SHARED_AT - SLAB)
                dve.wait_ge(gu_hi_done, q + 1)
                V.tensor_tensor(w_lo[:, slot, 0:SLAB_GU], w_all[:, bass.ds(at, SLAB_GU)],
                                w_hi[:, slot, 0:SLAB_GU].bitcast(F32), ALU.subtract).then_inc(gu_lo_done, 1)

            product(0, 0)
            for c in range(1, 4):
                product(c, c)
                lo_h(c - 1, c - 1)
                if c == 1:
                    weigh()
                if c == 2:
                    normalise()
                if c == 3:
                    dve.wait_ge(bias_prod_ready, 5)
                    choose_biases()

            def shared_pair(p, last):
                for c in range(4):
                    u = 4 * p + c
                    product(u, c)
                    lo_h(u - 1, (c - 1) % 4)
                    if c == ACC_AT:
                        add_acc(p - 1, PAIR, 4 * p)
                    if last and c >= 1:
                        lo_gate_up(c - 1, c - 1)

            with dve.Fori(1, PAIRS - 1) as p:
                shared_pair(p, False)
            dve.wait_ge(table_ready, 1)
            dve.wait_ge(d_experts, E * DMA)
            shared_pair(PAIRS - 1, True)

            def routed_batch(b, start):
                for j in range(4):
                    u = R0 + 4 * b + j
                    product(u, j, w_route[:, bass.ds(2 * b + j // 2, 1)])
                    lo_h(u - 1, (j - 1) % 4)
                    if j == ACC_AT:
                        if start:
                            add_acc(PAIRS - 1, PAIR, R0)
                        else:
                            add_acc(b - 1, S, R0 + 4 * b)
                    lo_gate_up(4 * b + j + 3, (j + 3) % 4)

            routed_batch(0, True)
            dve.wait_ge(d_l3, E // 2 * DMA)
            with dve.Fori(1, B) as b:
                routed_batch(b, False)

            def finish(t):
                dve.wait_ge(down_done, T0 + t + 1)
                at = slice(t * S, (t + 1) * S)
                V.scalar_tensor_tensor(x_in[:, at], acc(t, S), bias_b[:, 4, t:t + 1], x_res[:, at],
                                       ALU.add, ALU.add).then_inc(acc_read, 1)

            for t in range(B):
                u = T0 + t
                dve.wait_ge(act_done, u + 1)
                dve.wait_ge(up_ready, u + 1)
                full_slot_free(u)
                for c in range(2):
                    at = slice(c * S, (c + 1) * S)
                    last = V.scalar_tensor_tensor(h_full[:, t % 4, at], up_ps[t % 2][:, at],
                                                  bias_b[:, 2 + c, t:t + 1], h_act[:, t % 2, at],
                                                  ALU.add, ALU.mult)
                last.then_inc(prod_done, 1)
                lo_h(u - 1, (u - 1) % 4)
                if t == ACC_AT:
                    add_acc(B - 1, S, T0)
                if t > ACC_AT:
                    finish(t - ACC_AT - 1)
                if UNITS_ROUTED + t + 3 < PREPS:
                    lo_gate_up(UNITS_ROUTED + t + 3, (t + 3) % 4)
            lo_h(T0 + B - 1, (B - 1) % 4)
            for t in range(B - ACC_AT - 1, B):
                finish(t)


def constants():
    p = np.arange(P)
    c = np.zeros((P, C_COLS), np.float32)
    c[:, C_BLOCK:C_BLOCK + E] = p[:, None] // RANK == np.arange(E)
    c[:, C_DELTA:C_DELTA + RANK] = p[:, None] % RANK == np.arange(RANK)
    c[:, C_RANK:C_RANK + E] = E - np.arange(E)
    c[:, C_IDENT:] = np.eye(P)
    return c


def kernel(x, cond_8, L0_cond_weight, L0_cond_mask, L0_cond_bias, L1_cond_W_base, L1_cond_b_base,
           L1_cond_As, L1_cond_Bs, L2_cond_skill_gate, L2_cond_skill_up, L2_cond_skill_down,
           L2_cond_shared_gate, L2_cond_shared_up, L2_cond_shared_down, L3_cond_W_up, L3_cond_b_up,
           L3_cond_W_gate, L3_cond_b_gate, L3_cond_W_down, L3_cond_b_down):
    import concourse.bacc as bacc
    from concourse.bass_utils import run_bass_kernel_spmd

    a = np.asarray
    cat = np.concatenate

    def moe_slabs(gate, up, down):
        n = gate.shape[0]
        cols = [w.reshape(n, D, HALVES, 256).transpose(1, 0, 2, 3) for w in (gate, up)]
        rows = down.reshape(n, HALVES, 2, P, D).transpose(3, 0, 1, 2, 4).reshape(P, n, HALVES, 2 * D)
        return cat([*cols, rows], axis=3).reshape(P, n * HALVES * SLAB)

    up3, gate3 = (a(w).transpose(2, 0, 1) for w in (L3_cond_W_up, L3_cond_W_gate))
    down3 = a(L3_cond_W_down).transpose(2, 0, 1).reshape(2, P, E, D).transpose(1, 2, 0, 3).reshape(P, E, 2 * D)
    slabs = cat([
        moe_slabs(a(L2_cond_skill_gate), a(L2_cond_skill_up), a(L2_cond_skill_down)),
        cat([up3, gate3, down3], axis=2).reshape(P, E * SLAB),
        moe_slabs(a(L2_cond_shared_gate)[None], a(L2_cond_shared_up)[None], a(L2_cond_shared_down)[None]),
    ], axis=1)
    w_l0 = a(L0_cond_weight).reshape(E, D, TBLK, RANK).transpose(0, 3, 2, 1).reshape(P, TBLK, D)
    lin = np.stack([a(L0_cond_mask), a(L1_cond_As).reshape(P, D),
                    a(L1_cond_Bs).transpose(0, 2, 1).reshape(P, D), a(L1_cond_W_base).T], axis=1)
    chunks = [a(v).reshape(E, 2, P).transpose(2, 1, 0).reshape(P, 2 * E) for v in (L3_cond_b_up, L3_cond_b_gate)]
    vecs = cat([a(L0_cond_bias)[:, None], a(L1_cond_b_base)[:, None], *chunks, a(L3_cond_b_down).T], axis=1)
    data = {
        "xT": a(x).transpose(2, 0, 1).reshape(P, TOKENS), "cond": a(cond_8), "consts": constants(),
        "w_l0": w_l0, "lin": lin, "vecs": vecs, "slabs": slabs,
    }
    data = {k: np.ascontiguousarray(v) for k, v in data.items()}

    nc = bacc.Bacc("TRN2", target_bir_lowering=False, num_devices=1)
    args = {k: nc.dram_tensor(k, v.shape, F32, kind="ExternalInput").ap() for k, v in data.items()}
    outT = nc.dram_tensor("outT", (P, TOKENS), F32, kind="ExternalOutput").ap()
    build(nc, outT=outT, **args)
    r = run_bass_kernel_spmd(nc, [data], core_ids=[0])
    got = r.results[0]["outT"]
    return np.ascontiguousarray(got.reshape(P, B, S).transpose(1, 2, 0))
```

```python
from contextlib import ExitStack

import numpy as np

import concourse.bass as bass
from concourse import mybir

F32 = mybir.dt.float32
F32R = mybir.dt.float32r
I32 = mybir.dt.int32
ALU = mybir.AluOpType
ACT = mybir.ActivationFunctionType
AX_X = mybir.AxisListType.X

P = 128
B, S, D = 8, 256, 128
E = 8
RANK = 16
LORA_SCALE = 32.0 / RANK
I_MOE = 512
H_L3 = 256
TOKENS = B * S
PAIR = 2 * S
PAIRS = B // 2
SLAB = 3 * 256
SLAB_GU = 512
HALVES = I_MOE // 256
SLABS_EXPERTS = E * HALVES
SLABS_L3 = E
SHARED_AT = (SLABS_EXPERTS + SLABS_L3) * SLAB
SLABS = SLABS_EXPERTS + SLABS_L3 + HALVES
MOE_LAYER_SCALE = 1.0 / 12
TBLK = D // RANK

UNITS_SHARED = PAIRS * 4
UNITS_ROUTED = B * 4
PREPS = UNITS_ROUTED + B
R0 = UNITS_SHARED
T0 = UNITS_SHARED + UNITS_ROUTED
W_SLOTS = 4
H_SLOTS = 4
DOWN_LAG = 3
ACC_AT = 2
ACC_BIAS = 2
WARM_UP = 4
GU_DVE = 256
GU_DVE_L3 = 128
DVE_ROUNDS = 2
POOL_SUMS = range(2, 4)
OUT_GROUPS = ((0, 1), (1, 2), (2, 3), (4, 5), (3, 4), (5, 6), (6, 7), (7, 8))
DMA = 16

C_BLOCK = 0
C_DELTA = C_BLOCK + E
C_RANK = C_DELTA + RANK
C_IDENT = C_RANK + E
C_COLS = C_IDENT + P


def build(nc, xT, cond, consts, w_l0, lin, vecs, l0_bias, slabs, outT):
    with ExitStack() as ctx:
        def sb(name, shape, dt=F32):
            return ctx.enter_context(nc.sbuf_tensor(name, shape, dt))

        def bank(name):
            return ctx.enter_context(nc.psum_tensor(name, [P, 512], F32))

        def sem(name):
            return ctx.enter_context(nc.semaphore(name))

        w_all = sb("w_all", [P, SLABS * SLAB])
        x_in = sb("x_in", [P, TOKENS])
        cond_sb = sb("cond_sb", [P, B, E])
        const_sb = sb("const_sb", [P, C_COLS])
        w_l0_sb = sb("w_l0_sb", [P, TBLK, P])
        lin_sb = sb("lin_sb", [P, 4, P])
        bias_row = sb("bias_row", [P, P])
        vec_sb = sb("vec_sb", [P, 2 + 5 * E])
        block_of = const_sb[:, C_BLOCK:C_BLOCK + E]
        delta = const_sb[:, C_DELTA:C_DELTA + RANK]
        rank_e = const_sb[:, C_RANK:C_RANK + E]
        ident = const_sb[:, C_IDENT:C_IDENT + P]
        mask, lora_a, lora_bT, w_baseT = (lin_sb[:, k, :] for k in range(4))
        bias_l0, bias_l1 = vec_sb[:, 0:1], vec_sb[:, 1:2]
        bias_l3 = vec_sb[:, 2:].rearrange("p (k e) -> p k e", e=E)

        cond_blk = sb("cond_blk", [P, B, E])
        cond_row = sb("cond_row", [P, B])
        cond_scaled = sb("cond_scaled", [P, B])
        y_diag = sb("y_diag", [P, B, RANK])
        lora_bw = sb("lora_bw", [P, B, P])
        base_i = sb("base_i", [P, P])
        a_bias_prod = sb("a_bias_prod", [P, P])
        a_bias = sb("a_bias", [P, 1])
        a_bias_y = sb("a_bias_y", [P, B])
        w0_b = sb("w0_b", [P, B, P])
        r1_b = sb("r1_b", [P, B, P])
        m_b = sb("m_b", [P, B, P])
        c_b = sb("c_b", [P, B])
        x_res = sb("x_res", [P, TOKENS])
        x_hi = sb("x_hi", [P, TOKENS], F32R)
        x_lo = sb("x_lo", [P, TOKENS], F32R)

        top1 = sb("top1", [P, B])
        shifted = sb("shifted", [P, B, E])
        expd = sb("expd", [P, B, E])
        exp_sum = sb("exp_sum", [P, B])
        probs = sb("probs", [P, B, E])
        hit = sb("hit", [P, 2, B, E])
        key = sb("key", [P, B, E])
        first = sb("first", [P, 2, B])
        one_hot = sb("one_hot", [P, 2, B, E])
        rest = sb("rest", [P, B, E])
        top2 = sb("top2", [P, B])
        picked = sb("picked", [P, 2, B, E])
        w_pick = sb("w_pick", [P, 2, B])
        w_sum = sb("w_sum", [P, B])
        w_norm = sb("w_norm", [P, 2, B])
        w_part = sb("w_part", [P, 2, B])
        w_route = sb("w_route", [P, 2 * B])
        slab_at = sb("slab_at", [1, PREPS], I32)
        bias_prod = sb("bias_prod", [P, 5, B, E])
        bias_b = sb("bias_b", [P, 5, B])

        sh_hi = sb("sh_hi", [P, HALVES * SLAB], F32R)
        sh_lo = sb("sh_lo", [P, HALVES * SLAB], F32R)
        w_hi = sb("w_hi", [P, W_SLOTS, SLAB], F32R)
        w_lo = sb("w_lo", [P, W_SLOTS, SLAB], F32R)
        h_act = sb("h_act", [P, 2, 512])
        h_full = sb("h_full", [P, H_SLOTS, 512])
        h_hi = sb("h_hi", [P, H_SLOTS, 512], F32R)
        h_lo = sb("h_lo", [P, H_SLOTS, 512], F32R)
        zeros = sb("zeros", [P, S])
        table_first = sb("table_first", [P, 2])

        gate_ps = [bank("gate0"), bank("gate1")]
        up_ps = [bank("up0"), bank("up1")]
        acc_ps = ctx.enter_context(nc.psum_tensor("acc", [P, 2 * 512], F32))
        spare = [bank("spare0"), bank("spare1")]
        last_gate = [gate_ps[1][:, 0:S], gate_ps[0][:, 0:S]]
        last_up = [up_ps[1][:, 0:S], spare[1][:, 0:S]]
        m_banks = [gate_ps[0], up_ps[0], gate_ps[1], up_ps[1]]

        d_small, d_vecs, d_bias_row, d_lin = sem("d_small"), sem("d_vecs"), sem("d_bias_row"), sem("d_lin")
        d_w_l0, d_w_l0_second, d_x = sem("d_w_l0"), sem("d_w_l0_second"), sem("d_x")
        d_experts, d_l3 = sem("d_experts"), sem("d_l3")
        d_shared = [sem("d_shared0"), sem("d_shared1")]
        d_out = sem("d_out")
        dve_step, zeros_ready = sem("dve_step"), sem("zeros_ready")
        scaled_ready, bias_prod_ready = sem("scaled_ready"), sem("bias_prod_ready")
        y_ready, bw_ready, bw_ready_pool = sem("y_ready"), sem("bw_ready"), sem("bw_ready_pool")
        w0_sum, lora_sum = sem("w0_sum"), sem("lora_sum")
        w0_ready, r1_ready = sem("w0_ready"), sem("r1_ready")
        m_sum, m_ready = sem("m_sum"), sem("m_ready")
        a_bias_ready, c_sum = sem("a_bias_ready"), sem("c_sum")
        x2_sum, x2_ready, x2_second_ready, x2_hi, x2_lo_first, x2_lo = (
            sem(n) for n in ("x2_sum", "x2_ready", "x2_second_ready", "x2_hi", "x2_lo_first", "x2_lo"))
        shift_ready, exp_ready, table_ready = sem("shift_ready"), sem("exp_ready"), sem("table_ready")
        sh_hi_ready, sh_lo_ready = sem("sh_hi_ready"), sem("sh_lo_ready")
        gate_ready, up_ready = sem("gate_ready"), sem("up_ready")
        act_done, prod_done = sem("act_done"), sem("prod_done")
        h_hi_done, h_lo_done = sem("h_hi_done"), sem("h_lo_done")
        down_done = sem("down_done")
        acc_read = sem("acc_read")
        gu_hi_done, gu_lo_done, gu_lo_pool_done = sem("gu_hi_done"), sem("gu_lo_done"), sem("gu_lo_pool_done")
        wd_hi_done, wd_lo_done = sem("wd_hi_done"), sem("wd_lo_done")
        summed = sem("summed")
        x3_hi, x3_lo = sem("x3_hi"), sem("x3_lo")

        block = ctx.enter_context(nc.Block())

        def acc(group, n):
            return acc_ps[:, bass.ds((group % 2) * 512, n)]

        def l3_acc(t):
            return (acc(0, S), acc(1, S), spare[0][:, 0:S])[t % 3]

        def slab_of(engine, q):
            return engine.value_load(slab_at[0:1, bass.ds(q, 1)], min_val=0, max_val=SHARED_AT - SLAB)

        def x2_ps(b):
            if b < 2:
                return spare[b][:, 0:S]
            return (acc_ps[:, 512:1024], spare[0], spare[1])[b // 2 - 1][:, (b % 2) * S:(b % 2 + 1) * S]

        def rows(ap, b):
            return ap.unsqueeze(1).to_broadcast([P, b, ap.shape[-1]])

        @block.sync
        def _(sp):
            sp.dma_start(cond_sb[:, :, :], cond.unsqueeze(0).to_broadcast([P, B, E])).then_inc(d_small, DMA)
            sp.dma_start(const_sb[:, :], consts).then_inc(d_small, DMA)
            sp.dma_start(w_l0_sb[:, 0:4, :], w_l0[:, 0:4, :]).then_inc(d_w_l0, DMA)
            sp.dma_start(lin_sb[:, :, :], lin).then_inc(d_lin, DMA)
            sp.dma_start(w_l0_sb[:, 4:8, :], w_l0[:, 4:8, :]).then_inc(d_w_l0_second, DMA)
            sp.dma_start(bias_row[:, :], l0_bias.unsqueeze(0).to_broadcast([P, P])).then_inc(d_bias_row, DMA)
            sp.dma_start(vec_sb[:, :], vecs).then_inc(d_vecs, DMA)
            sp.dma_start(x_in[:, :], xT).then_inc(d_x, DMA)
            for k, arrived in enumerate(d_shared):
                at = slice(SHARED_AT + k * SLAB, SHARED_AT + (k + 1) * SLAB)
                sp.dma_start(w_all[:, at], slabs[:, at]).then_inc(arrived, DMA)
            for e in range(E):
                at = slice(e * HALVES * SLAB, (e + 1) * HALVES * SLAB)
                sp.dma_start(w_all[:, at], slabs[:, at]).then_inc(d_experts, DMA)
            for e in range(0, E, 2):
                at = slice((SLABS_EXPERTS + e) * SLAB, (SLABS_EXPERTS + e + 2) * SLAB)
                sp.dma_start(w_all[:, at], slabs[:, at]).then_inc(d_l3, DMA)
            for first_b, after_b in OUT_GROUPS:
                last_b = after_b - 1
                if last_b in POOL_SUMS:
                    sp.wait_ge(summed, last_b - POOL_SUMS[0] + 1)
                else:
                    sp.wait_ge(acc_read, ACC_BIAS + PAIRS + B + last_b + 1)
                at = slice(first_b * S, after_b * S)
                sp.dma_start(outT[:, at], x_in[:, at]).then_inc(d_out, DMA)
            sp.wait_ge(d_out, len(OUT_GROUPS) * DMA)

        @block.tensor
        def _(pe):
            def mm(out, lhsT, rhs, start, stop):
                return nc.tensor.matmul(out, lhsT, rhs, start=start, stop=stop)

            def split_product(out, a_hi, a_lo, b_hi, b_lo, start=True, stop=True):
                mm(out, a_hi, b_hi, start, False)
                mm(out, a_hi, b_lo, False, False)
                return mm(out, a_lo, b_hi, False, stop)

            pe.wait_ge(zeros_ready, 1)
            for _ in range(WARM_UP):
                mm(acc_ps[:, 0:S], zeros[:, 0:P], zeros[:], True, True)
            pe.wait_ge(y_ready, 1)
            for k in range(2):
                pe.wait_ge((d_w_l0, d_w_l0_second)[k], DMA)
                for i in range(4):
                    last = mm(spare[k][:, i * P:(i + 1) * P], w_l0_sb[:, 4 * k + i, :],
                              y_diag[:].rearrange("p b t -> p (b t)"), True, True)
                last.then_inc(w0_sum, 1)
                pe.wait_ge((bw_ready, bw_ready_pool)[k], 1)
                mm(gate_ps[k][:], lora_a, lora_bw[:, 4 * k:4 * k + 4, :].rearrange("p b o -> p (b o)"),
                   True, True).then_inc(lora_sum, 1)
            pe.wait_ge(d_vecs, DMA)
            pe.wait_ge(a_bias_ready, 1)
            mm(acc_ps[:, 0:B], base_i[:], bias_l0.to_broadcast([P, B]), True, False)
            mm(acc_ps[:, 0:B], lora_bT, a_bias_y[:], False, True).then_inc(c_sum, 1)

            def matrix(p):
                pe.wait_ge(r1_ready, p // 2 + 1)
                pe.wait_ge(w0_ready, 2)
                for b in (2 * p, 2 * p + 1):
                    at = (b % 2) * P
                    last = mm(m_banks[p][:, at:at + P], w0_b[:, b, :], r1_b[:, b, :], True, True)
                last.then_inc(m_sum, 1)

            for p in range(3):
                matrix(p)
            pe.wait_ge(d_x, DMA)

            def x2(p):
                pe.wait_ge(m_ready, p + 1)
                if p == 2:
                    pe.wait_ge(x2_ready, 1)
                if p == 3:
                    pe.wait_ge(x2_second_ready, 1)
                for k in range(2):
                    b = 2 * p + k
                    last = mm(x2_ps(b), m_b[:, b, :],
                              x_in[:, b * S:(b + 1) * S], True, True)
                last.then_inc(x2_sum, 1)

            def acts_until(u):
                return T0 + 2 * (u - T0) if isinstance(u, int) and u > T0 else u

            def banks_free(u, first_use):
                if not first_use:
                    pe.wait_ge(act_done, acts_until(u - 1))
                    pe.wait_ge(prod_done, u - 1)

            def shared_up(p, c, first_use=False):
                u = 4 * p + c
                banks_free(u, first_use)
                at = (c // 2) * SLAB + (c % 2) * P
                tok = bass.ds(p * PAIR, PAIR)
                for out, off, done in ((gate_ps[c % 2], 0, gate_ready), (up_ps[c % 2], 256, up_ready)):
                    w = slice(at + off, at + off + P)
                    split_product(out[:], sh_hi[:, w], sh_lo[:, w], x_hi[:, tok], x_lo[:, tok]).then_inc(done, 1)

            def first_shared_up():
                pe.wait_ge(x2_hi, 1)
                parts = ((gate_ps[0], slice(0, P), gate_ready), (up_ps[0], slice(256, 256 + P), up_ready))
                for out, w, _ in parts:
                    mm(out[:], sh_hi[:, w], x_hi[:, 0:PAIR], True, False)
                    mm(out[:], sh_lo[:, w], x_hi[:, 0:PAIR], False, False)
                pe.wait_ge(x2_lo_first, 1)
                for out, w, done in parts:
                    mm(out[:], sh_hi[:, w], x_lo[:, 0:PAIR], False, True).then_inc(done, 1)

            def hidden_split(u):
                pe.wait_ge(h_hi_done, u + 1)
                pe.wait_ge(h_lo_done, u + 1)

            def acc_bank_free(group):
                pe.wait_ge(acc_read, group + 1)

            def shared_down(p, c):
                u = 4 * p + c
                hidden_split(u)
                if c == 0:
                    acc_bank_free(p)
                at = (c // 2) * SLAB + SLAB_GU + (c % 2) * P
                w = slice(at, at + P)
                split_product(acc(p, 512), sh_hi[:, w], sh_lo[:, w], h_hi[:, c, :], h_lo[:, c, :],
                              c == 0, c == 3).then_inc(down_done, 1)

            def slab_up(u, q, slot, b):
                banks_free(u, False)
                pe.wait_ge(gu_hi_done, q + 1)
                pe.wait_ge(gu_lo_done, q + 1)
                pe.wait_ge(gu_lo_pool_done, q + 1)
                tok = bass.ds(b * S, S)
                for out, off, done in ((gate_ps[slot % 2], 0, gate_ready), (up_ps[slot % 2], 256, up_ready)):
                    for c in range(2):
                        w = slice(off + c * P, off + (c + 1) * P)
                        last = split_product(out[:, c * S:(c + 1) * S], w_hi[:, slot, w], w_lo[:, slot, w],
                                             x_hi[:, tok], x_lo[:, tok])
                    last.then_inc(done, 1)

            def slab_down(u, q, slot, out, start, stop):
                hidden_split(u)
                pe.wait_ge(wd_hi_done, q + 1)
                pe.wait_ge(wd_lo_done, q + 1)
                for c in range(2):
                    w = slice(SLAB_GU + c * P, SLAB_GU + (c + 1) * P)
                    h = slice(c * S, (c + 1) * S)
                    last = split_product(out, w_hi[:, slot, w], w_lo[:, slot, w],
                                         h_hi[:, slot, h], h_lo[:, slot, h],
                                         start and c == 0, stop and c == 1)
                last.then_inc(down_done, 1)

            def routed_down(b, j):
                if j == 0:
                    acc_bank_free(PAIRS + b)
                slab_down(R0 + 4 * b + j, 4 * b + j, j, acc(b, S), j == 0, j == 3)

            x2(0)
            matrix(3)
            x2(1)
            for c in range(4):
                pe.wait_ge(sh_hi_ready, c // 2 + 1)
                pe.wait_ge(sh_lo_ready, c // 2 + 1)
                if c < 2:
                    pe.wait_ge(m_ready, 2 * (c + 1))
                if c == 0:
                    first_shared_up()
                else:
                    shared_up(0, c, first_use=c < 2)
                if c + 2 < PAIRS:
                    x2(c + 2)
                if c >= DOWN_LAG:
                    shared_down(0, c - DOWN_LAG)
            with pe.Fori(1, PAIRS) as p:
                pe.wait_ge(x2_hi, p + 1)
                pe.wait_ge(x2_lo, p)
                for c in range(4):
                    shared_up(p, c)
                    shared_down(p if c >= DOWN_LAG else p - 1, (c - DOWN_LAG) % 4)

            for j in range(4):
                slab_up(R0 + j, j, j, 0)
                if j < DOWN_LAG:
                    shared_down(PAIRS - 1, 4 + j - DOWN_LAG)
                else:
                    routed_down(0, j - DOWN_LAG)
            with pe.Fori(1, B) as b:
                for j in range(4):
                    slab_up(R0 + 4 * b + j, 4 * b + j, j, b)
                    routed_down(b if j >= DOWN_LAG else b - 1, (j - DOWN_LAG) % 4)

            def l3_down(t):
                if t < 2:
                    acc_bank_free(PAIRS + B + t)
                elif t >= 3:
                    pe.wait_ge(acc_read, ACC_BIAS + PAIRS + B + t - 2)
                slab_down(T0 + t, UNITS_ROUTED + t, t % 4, l3_acc(t), True, True)

            def last_gate_up():
                t = B - 1
                q = UNITS_ROUTED + t
                banks_free(T0 + t, False)
                pe.wait_ge(gu_hi_done, q + 1)
                pe.wait_ge(gu_lo_done, q + 1)
                pe.wait_ge(gu_lo_pool_done, q + 1)
                tok = slice(t * S, (t + 1) * S)
                for c in range(2):
                    if c == 1:
                        pe.wait_ge(act_done, acts_until(T0 + t))
                    for out, off, done in ((last_gate[c], 0, gate_ready), (last_up[c], 256, up_ready)):
                        w = slice(off + c * P, off + (c + 1) * P)
                        split_product(out, w_hi[:, t % 4, w], w_lo[:, t % 4, w],
                                      x_hi[:, tok], x_lo[:, tok]).then_inc(done, 1)

            def last_down():
                t = B - 1
                pe.wait_ge(acc_read, ACC_BIAS + PAIRS + B + t - 2)
                pe.wait_ge(wd_hi_done, PREPS)
                pe.wait_ge(wd_lo_done, PREPS)
                for c in range(2):
                    pe.wait_ge(h_hi_done, T0 + t + 1 + c)
                    pe.wait_ge(h_lo_done, T0 + t + 1 + c)
                    w = slice(SLAB_GU + c * P, SLAB_GU + (c + 1) * P)
                    h = slice(c * S, (c + 1) * S)
                    last = split_product(l3_acc(t), w_hi[:, t % 4, w], w_lo[:, t % 4, w],
                                         h_hi[:, t % 4, h], h_lo[:, t % 4, h], c == 0, c == 1)
                last.then_inc(down_done, 1)

            for t in range(B):
                pe.wait_ge(x3_hi, t + 1)
                pe.wait_ge(x3_lo, t + 1)
                if t == B - 1:
                    last_gate_up()
                else:
                    slab_up(T0 + t, UNITS_ROUTED + t, t % 4, t)
                if t < DOWN_LAG:
                    routed_down(B - 1, 4 + t - DOWN_LAG)
                else:
                    l3_down(t - DOWN_LAG)
            for t in range(B - DOWN_LAG, B - 1):
                l3_down(t)
            last_down()

        @block.scalar
        def _(act):
            act.wait_ge(shift_ready, 1)
            nc.scalar.activation(expd[:], shifted[:], ACT.Exp).then_inc(exp_ready, 1)
            nc.scalar.activation(table_first[:, 0:1], cond_sb[:, 0, 0:1], ACT.Gelu_apprx_tanh)

            def round_shared(k):
                act.wait_ge(d_shared[k], DMA)
                at = slice(k * SLAB, (k + 1) * SLAB)
                nc.scalar.activation(sh_hi[:, at], w_all[:, SHARED_AT + k * SLAB:SHARED_AT + (k + 1) * SLAB],
                                     ACT.Copy).then_inc(sh_hi_ready, 1)

            def x2(p):
                act.wait_ge(x2_sum, p + 1)
                act.wait_ge(acc_read, ACC_BIAS)
                for b in (2 * p, 2 * p + 1) if p else (0,):
                    last = nc.scalar.activation(x_res[:, b * S:(b + 1) * S], x2_ps(b),
                                                ACT.Identity, bias=c_b[:, b:b + 1])
                last.then_inc(x2_ready, 1)
                act.wait_ge(x2_ready, p + 1)
                if p == 0:
                    act.wait_ge(x2_second_ready, 1)
                at = slice(p * PAIR, (p + 1) * PAIR)
                nc.scalar.activation(x_hi[:, at], x_res[:, at], ACT.Copy).then_inc(x2_hi, 1)

            round_shared(0)
            x2(0)
            round_shared(1)
            x2(1)

            def gelu(u, k):
                act.wait_ge(gate_ready, u + 1)
                if not (isinstance(u, int) and u < 2):
                    act.wait_ge(prod_done, u - 1)
                nc.scalar.activation(h_act[:, k, :], gate_ps[k][:], ACT.Gelu_apprx_tanh).then_inc(act_done, 1)

            def round_h(u, slot):
                act.wait_ge(prod_done, u + 1)
                if not (isinstance(u, int) and u < H_SLOTS):
                    act.wait_ge(down_done, u + 1 - H_SLOTS)
                nc.scalar.activation(h_hi[:, slot, :], h_full[:, slot, :], ACT.Copy).then_inc(h_hi_done, 1)

            def round_gate_up(q, slot):
                at = slab_of(act, q)
                if not (isinstance(q, int) and q < W_SLOTS):
                    act.wait_ge(up_ready, q + R0 + 1 - W_SLOTS)
                nc.scalar.activation(w_hi[:, slot, 0:SLAB_GU], w_all[:, bass.ds(at, SLAB_GU)],
                                     ACT.Copy).then_inc(gu_hi_done, 1)

            def round_down(q, slot):
                at = slab_of(act, q)
                if not (isinstance(q, int) and q < W_SLOTS):
                    act.wait_ge(down_done, q + R0 + 1 - W_SLOTS)
                nc.scalar.activation(w_hi[:, slot, SLAB_GU:], w_all[:, bass.ds(at + SLAB_GU, SLAB - SLAB_GU)],
                                     ACT.Copy).then_inc(wd_hi_done, 1)

            gelu(0, 0)
            for c in range(1, 4):
                gelu(c, c % 2)
                round_h(c - 1, c - 1)
                if c + 1 < PAIRS:
                    x2(c + 1)
            with act.Fori(1, PAIRS - 1) as p:
                for c in range(4):
                    gelu(4 * p + c, c % 2)
                    round_h(4 * p + c - 1, (c - 1) % 4)
            act.wait_ge(table_ready, 1)
            act.wait_ge(d_experts, E * DMA)
            for c in range(4):
                u = 4 * (PAIRS - 1) + c
                gelu(u, u % 2)
                round_h(u - 1, (u - 1) % 4)
                if c >= 1:
                    round_gate_up(c - 1, c - 1)
                if c == 3:
                    round_down(0, 0)

            def routed_batch(b):
                for j in range(4):
                    u = R0 + 4 * b + j
                    gelu(u, j % 2)
                    round_h(u - 1, (j - 1) % 4)
                    round_gate_up(4 * b + j + 3, (j + 3) % 4)
                    round_down(4 * b + j + 1, (j + 1) % 4)

            routed_batch(0)
            act.wait_ge(d_l3, E // 2 * DMA)
            with act.Fori(1, B) as b:
                routed_batch(b)

            def add_bias(t):
                act.wait_ge(down_done, T0 + t + 1)
                act.wait_ge(acc_read, ACC_BIAS + PAIRS + B + t)
                nc.scalar.activation(x_in[:, t * S:(t + 1) * S], l3_acc(t), ACT.Identity,
                                     bias=bias_b[:, 4, t:t + 1]).then_inc(acc_read, 1)

            nc.scalar.activation(table_first[:, 1:2], cond_sb[:, 0, 0:1], ACT.Silu)
            for t in range(B - 1):
                u = T0 + t
                act.wait_ge(gate_ready, u + 1)
                act.wait_ge(prod_done, u - 1)
                for c in range(2):
                    nc.scalar.activation(h_act[:, t % 2, c * S:(c + 1) * S],
                                         gate_ps[t % 2][:, c * S:(c + 1) * S], ACT.Silu,
                                         bias=bias_b[:, c, t:t + 1]).then_inc(act_done, 1)
                round_h(u - 1, (u - 1) % 4)
                if UNITS_ROUTED + t + 3 < PREPS:
                    round_gate_up(UNITS_ROUTED + t + 3, (t + 3) % 4)
                if t == DVE_ROUNDS:
                    act.wait_ge(wd_hi_done, UNITS_ROUTED + 1 + DVE_ROUNDS)
                if DVE_ROUNDS <= t < B - 2:
                    round_down(UNITS_ROUTED + t + 1, (t + 1) % 4)
            t = B - 1
            u = T0 + t
            act.wait_ge(prod_done, u - 1)
            for c in range(2):
                act.wait_ge(gate_ready, u + 1 + c)
                nc.scalar.activation(h_act[:, t % 2, c * S:(c + 1) * S], last_gate[c], ACT.Silu,
                                     bias=bias_b[:, c, t:t + 1]).then_inc(act_done, 1)
                if c == 0:
                    add_bias(2)
                    round_h(u - 1, (u - 1) % 4)
                    round_down(PREPS - 1, (B - 1) % 4)
            add_bias(3)
            act.wait_ge(down_done, u + 1 - H_SLOTS)
            for c in range(2):
                act.wait_ge(prod_done, u + 1 + c)
                h = slice(c * S, (c + 1) * S)
                nc.scalar.activation(h_hi[:, t % 4, h], h_full[:, t % 4, h], ACT.Copy).then_inc(h_hi_done, 1)

        @block.gpsimd
        def _(pool):
            pool.wait_ge(scaled_ready, 1)
            pool.wait_ge(d_lin, DMA)
            nc.gpsimd.tensor_tensor(lora_bw[:, 4:8], rows(lora_bT, 4),
                                    cond_scaled[:, 4:8].unsqueeze(2).to_broadcast([P, 4, P]),
                                    ALU.mult).then_inc(bw_ready_pool, 1)
            for k in range(HALVES):
                pool.wait_ge(d_shared[k], DMA)
                at = slice(k * SLAB, (k + 1) * SLAB)
                pool.wait_ge(sh_hi_ready, k + 1)
                nc.gpsimd.tensor_tensor(sh_lo[:, at], w_all[:, SHARED_AT + k * SLAB:SHARED_AT + (k + 1) * SLAB],
                                        sh_hi[:, at].bitcast(F32), ALU.subtract).then_inc(sh_lo_ready, 1)
            for p in range(1, PAIRS):
                pool.wait_ge(x2_hi, p + 1)
                at = slice(p * PAIR, (p + 1) * PAIR)
                nc.gpsimd.tensor_tensor(x_lo[:, at], x_res[:, at], x_hi[:, at].bitcast(F32),
                                        ALU.subtract).then_inc(x2_lo, 1)

            pool.wait_ge(table_ready, 1)
            pool.wait_ge(d_vecs, DMA)
            for k in range(5):
                nc.gpsimd.tensor_tensor(bias_prod[:, k], rows(bias_l3[:, k], B), one_hot[:, 0],
                                        ALU.mult).then_inc(bias_prod_ready, 1)

            def lo_down(q, slot):
                at = slab_of(pool, q)
                pool.wait_ge(wd_hi_done, q + 1)
                nc.gpsimd.tensor_tensor(w_lo[:, slot, SLAB_GU:], w_all[:, bass.ds(at + SLAB_GU, SLAB - SLAB_GU)],
                                        w_hi[:, slot, SLAB_GU:].bitcast(F32), ALU.subtract).then_inc(wd_lo_done, 1)

            def lo_gate_up(q, slot, split=GU_DVE):
                at = slab_of(pool, q)
                pool.wait_ge(gu_hi_done, q + 1)
                n = SLAB_GU - split
                nc.gpsimd.tensor_tensor(w_lo[:, slot, split:SLAB_GU], w_all[:, bass.ds(at + split, n)],
                                        w_hi[:, slot, split:SLAB_GU].bitcast(F32),
                                        ALU.subtract).then_inc(gu_lo_pool_done, 1)

            def lo_x3(b):
                pool.wait_ge(x3_hi, b + 1)
                at = bass.ds(b * S, S)
                nc.gpsimd.tensor_tensor(x_lo[:, at], x_res[:, at], x_hi[:, at].bitcast(F32),
                                        ALU.subtract).then_inc(x3_lo, 1)

            pool.wait_ge(table_ready, 1)
            pool.wait_ge(d_experts, E * DMA)
            for q in range(3):
                lo_gate_up(q, q)
            lo_down(0, 0)
            for q in range(4):
                lo_gate_up(q + 3, (q + 3) % 4)
                lo_down(q + 1, (q + 1) % 4)
            pool.wait_ge(d_l3, E // 2 * DMA)
            with pool.Fori(1, B) as b:
                for j in range(4):
                    lo_gate_up(4 * b + j + 3, (j + 3) % 4)
                    lo_down(4 * b + j + 1, (j + 1) % 4)
                    if j == 3:
                        lo_x3(b - 1)

            def add_residual(t):
                pool.wait_ge(acc_read, ACC_BIAS + PAIRS + B + t + 1)
                at = slice(t * S, (t + 1) * S)
                nc.gpsimd.tensor_tensor(x_in[:, at], x_in[:, at], x_res[:, at], ALU.add).then_inc(summed, 1)

            for q in range(UNITS_ROUTED + 1, PREPS):
                if q == PREPS - 1:
                    add_residual(2)
                if q + 2 < PREPS:
                    lo_gate_up(q + 2, (q + 2) % 4, GU_DVE_L3)
                lo_down(q, q % 4)
                if q == UNITS_ROUTED + 4:
                    lo_x3(B - 1)
            add_residual(3)

        @block.vector
        def _(dve):
            V = nc.vector
            steps = [0]

            def then(ins):
                steps[0] += 1
                ins.then_inc(dve_step, 1)
                dve.wait_ge(dve_step, steps[0])

            def over_e(ap):
                return ap.unsqueeze(2).to_broadcast([P, B, E])

            def choose():
                then(V.tensor_tensor(hit[:, 0], cond_sb[:], over_e(top1[:]), ALU.is_equal))
                then(V.tensor_tensor(key[:], hit[:, 0], rows(rank_e, B), ALU.mult))
                then(V.tensor_reduce(first[:, 0], key[:], AX_X, ALU.max))
                then(V.tensor_tensor(one_hot[:, 0], rows(rank_e, B), over_e(first[:, 0]), ALU.is_equal))

            def choose_second():
                then(V.scalar_tensor_tensor(rest[:], one_hot[:, 0], -3.0e38, cond_sb[:], ALU.mult, ALU.add))
                then(V.tensor_reduce(top2[:], rest[:], AX_X, ALU.max))
                then(V.tensor_tensor(hit[:, 1], rest[:], over_e(top2[:]), ALU.is_equal))
                then(V.tensor_tensor(key[:], hit[:, 1], rows(rank_e, B), ALU.mult))
                then(V.tensor_reduce(first[:, 1], key[:], AX_X, ALU.max))
                then(V.tensor_tensor(one_hot[:, 1], rows(rank_e, B), over_e(first[:, 1]), ALU.is_equal))

            def weigh():
                dve.wait_ge(exp_ready, 1)
                then(V.tensor_reduce(exp_sum[:], expd[:], AX_X, ALU.add))
                then(V.reciprocal(exp_sum[:], exp_sum[:]))
                then(V.tensor_tensor(probs[:], expd[:], over_e(exp_sum[:]), ALU.mult))
                then(V.tensor_tensor(picked[:].rearrange("p k b e -> p k (b e)"),
                                     one_hot[:].rearrange("p k b e -> p k (b e)"),
                                     rows(probs[:].rearrange("p b e -> p (b e)"), 2), ALU.mult))
                then(V.tensor_reduce(w_pick[:], picked[:], AX_X, ALU.add))

            def normalise():
                then(V.tensor_tensor(w_sum[:], w_pick[:, 0], w_pick[:, 1], ALU.add))
                then(V.reciprocal(w_sum[:], w_sum[:]))
                then(V.tensor_tensor(w_norm[:], w_pick[:], rows(w_sum[:], 2), ALU.mult))
                then(V.tensor_scalar(w_part[:], w_norm[:], 1.0 - MOE_LAYER_SCALE, None, ALU.mult))
                then(V.scalar_tensor_tensor(w_route[:].rearrange("p (b k) -> p k b", k=2), w_norm[:],
                                            MOE_LAYER_SCALE, w_part[:], ALU.mult, ALU.add))

            def tabulate():
                table = slab_at[0:1, 0:UNITS_ROUTED].rearrange("p (b k h) -> p k b h", k=2, h=HALVES)
                for k in range(2):
                    for h in range(HALVES):
                        V.tensor_scalar(table[:, k, :, h], first[0:1, k], -float(HALVES * SLAB),
                                        float((E * HALVES + h) * SLAB), ALU.mult, ALU.add)
                V.tensor_scalar(slab_at[0:1, UNITS_ROUTED:], first[0:1, 0], -float(SLAB),
                                float((SLABS_EXPERTS + E) * SLAB), ALU.mult, ALU.add).then_inc(table_ready, 1)

            def choose_biases():
                then(V.tensor_reduce(bias_b[:], bias_prod[:], AX_X, ALU.add))

            V.memset(zeros[:], 0.0).then_inc(zeros_ready, 1)
            dve.wait_ge(d_small, 2 * DMA)
            then(V.tensor_tensor(cond_blk[:], cond_sb[:], rows(block_of, B), ALU.mult))
            then(V.tensor_reduce(cond_row[:], cond_blk[:], AX_X, ALU.add))
            V.tensor_tensor(y_diag[:], cond_row[:].unsqueeze(2).to_broadcast([P, B, RANK]),
                            rows(delta, B), ALU.mult).then_inc(y_ready, 1)
            V.tensor_scalar(cond_scaled[:], cond_row[:], LORA_SCALE, None, ALU.mult).then_inc(scaled_ready, 1)
            then(V.tensor_reduce(top1[:], cond_sb[:], AX_X, ALU.max))
            V.tensor_tensor(shifted[:], cond_sb[:], over_e(top1[:]), ALU.subtract).then_inc(shift_ready, 1)
            choose()
            dve.wait_ge(d_lin, DMA)
            dve.wait_ge(scaled_ready, 1)
            V.tensor_tensor(lora_bw[:, 0:4], rows(lora_bT, 4),
                            cond_scaled[:, 0:4].unsqueeze(2).to_broadcast([P, 4, P]),
                            ALU.mult).then_inc(bw_ready, 1)
            V.tensor_tensor(base_i[:], ident, w_baseT, ALU.add)
            dve.wait_ge(d_bias_row, DMA)
            then(V.tensor_tensor(a_bias_prod[:], lora_a, bias_row[:], ALU.mult))
            then(V.tensor_reduce(a_bias[:], a_bias_prod[:], AX_X, ALU.add))
            V.tensor_scalar(a_bias_y[:], cond_scaled[:], a_bias[:], None, ALU.mult).then_inc(a_bias_ready, 1)
            for k in range(2):
                dve.wait_ge(w0_sum, k + 1)
                kk = slice(4 * k, 4 * k + 4)
                V.tensor_tensor(
                    w0_b[:].rearrange("o b (k t) -> o k b t", t=RANK)[:, kk],
                    spare[k][:].rearrange("o (k b t) -> o k b t", k=4, t=RANK),
                    mask.rearrange("o (k t) -> o k t", t=RANK)[:, kk].unsqueeze(2).to_broadcast([P, 4, B, RANK]),
                    ALU.mult).then_inc(w0_ready, 1)
                dve.wait_ge(lora_sum, k + 1)
                V.tensor_tensor(r1_b[:, 4 * k:4 * k + 4, :], gate_ps[k][:].rearrange("c (b o) -> c b o", b=4),
                                rows(base_i[:], 4), ALU.add).then_inc(r1_ready, 1)
            dve.wait_ge(r1_ready, 2)
            dve.wait_ge(d_vecs, DMA)
            dve.wait_ge(c_sum, 1)
            V.tensor_scalar(c_b[:], acc_ps[:, 0:B], bias_l1, None, ALU.add).then_inc(acc_read, ACC_BIAS)
            for k in range(PAIRS):
                dve.wait_ge(m_sum, k + 1)
                bb = slice(2 * k, 2 * k + 2)
                V.tensor_tensor(m_b[:, bb, :],
                                m_banks[k][:, 0:2 * P].rearrange("c (b o) -> c b o", b=2),
                                r1_b[:, bb, :], ALU.add).then_inc(m_ready, 1)
                if k == 1:
                    dve.wait_ge(x2_sum, 1)
                    V.tensor_scalar(x_res[:, S:2 * S], x2_ps(1), c_b[:, 1:2], None,
                                    ALU.add).then_inc(x2_second_ready, 1)
                if k == 2:
                    dve.wait_ge(x2_hi, 1)
                    V.tensor_tensor(x_lo[:, 0:PAIR], x_res[:, 0:PAIR], x_hi[:, 0:PAIR].bitcast(F32),
                                    ALU.subtract).then_inc(x2_lo_first, 1)
            choose_second()
            tabulate()

            def lo_h(u, slot):
                dve.wait_ge(h_hi_done, u + 1)
                V.tensor_tensor(h_lo[:, slot, :], h_full[:, slot, :], h_hi[:, slot, :].bitcast(F32),
                                ALU.subtract).then_inc(h_lo_done, 1)

            def full_slot_free(u):
                if not (isinstance(u, int) and u < H_SLOTS):
                    dve.wait_ge(h_lo_done, u + 1 - H_SLOTS)

            def product(u, slot, weight=None):
                k = slot % 2
                full_slot_free(u)
                dve.wait_ge(act_done, u + 1)
                dve.wait_ge(up_ready, u + 1)
                if weight is None:
                    ins = V.tensor_tensor(h_full[:, slot, :], h_act[:, k, :], up_ps[k][:], ALU.mult)
                else:
                    ins = V.scalar_tensor_tensor(h_full[:, slot, :], h_act[:, k, :], weight, up_ps[k][:],
                                                 ALU.mult, ALU.mult)
                ins.then_inc(prod_done, 1)

            def add_acc(group, n, down):
                at = group * n
                dve.wait_ge(down_done, down)
                V.tensor_tensor(x_res[:, bass.ds(at, n)], acc(group, n), x_res[:, bass.ds(at, n)],
                                ALU.add).then_inc(acc_read, 1)

            def round_x3(b):
                dve.wait_ge(acc_read, ACC_BIAS + PAIRS + b + 1)
                at = bass.ds(b * S, S)
                V.tensor_copy(x_hi[:, at], x_res[:, at]).then_inc(x3_hi, 1)

            def lo_gate_up(q, slot, at=None, split=GU_DVE):
                if at is None:
                    at = slab_of(dve, q)
                dve.wait_ge(gu_hi_done, q + 1)
                V.tensor_tensor(w_lo[:, slot, 0:split], w_all[:, bass.ds(at, split)],
                                w_hi[:, slot, 0:split].bitcast(F32), ALU.subtract).then_inc(gu_lo_done, 1)

            product(0, 0)
            weigh()
            for c in range(1, 4):
                product(c, c)
                lo_h(c - 1, c - 1)

            def shared_pair(p, last):
                for c in range(4):
                    u = 4 * p + c
                    product(u, c)
                    lo_h(u - 1, (c - 1) % 4)
                    if last and c == 0:
                        normalise()
                    if last and c == 3:
                        dve.wait_ge(bias_prod_ready, 5)
                        choose_biases()
                    if c == ACC_AT:
                        add_acc(p - 1, PAIR, 4 * p)
                    if last and c >= 1:
                        lo_gate_up(c - 1, c - 1)

            with dve.Fori(1, PAIRS - 1) as p:
                shared_pair(p, False)
            dve.wait_ge(table_ready, 1)
            dve.wait_ge(d_experts, E * DMA)
            shared_pair(PAIRS - 1, True)

            def routed_batch(b, start):
                for j in range(4):
                    u = R0 + 4 * b + j
                    product(u, j, w_route[:, bass.ds(2 * b + j // 2, 1)])
                    lo_h(u - 1, (j - 1) % 4)
                    if j == ACC_AT:
                        if start:
                            add_acc(PAIRS - 1, PAIR, R0)
                        else:
                            add_acc(b - 1, S, R0 + 4 * b)
                    if j == 3 and not start:
                        round_x3(b - 1)
                    lo_gate_up(4 * b + j + 3, (j + 3) % 4)

            routed_batch(0, True)
            dve.wait_ge(d_l3, E // 2 * DMA)
            with dve.Fori(1, B) as b:
                routed_batch(b, False)

            def round_down(q, at):
                dve.wait_ge(wd_hi_done, q)
                dve.wait_ge(down_done, q + R0 + 1 - W_SLOTS)
                V.tensor_copy(w_hi[:, q % 4, SLAB_GU:],
                              w_all[:, bass.ds(at + SLAB_GU, SLAB - SLAB_GU)]).then_inc(wd_hi_done, 1)

            def finish(t):
                dve.wait_ge(down_done, T0 + t + 1)
                at = slice(t * S, (t + 1) * S)
                V.scalar_tensor_tensor(x_in[:, at], l3_acc(t), bias_b[:, 4, t:t + 1], x_res[:, at],
                                       ALU.add, ALU.add).then_inc(acc_read, 1)

            down_at = [slab_of(dve, UNITS_ROUTED + t + 1) for t in range(DVE_ROUNDS)]
            for t in range(B - 1):
                u = T0 + t
                dve.wait_ge(up_ready, u + 1)
                full_slot_free(u)
                for c in range(2):
                    dve.wait_ge(act_done, T0 + 2 * t + c + 1)
                    at = slice(c * S, (c + 1) * S)
                    last = V.scalar_tensor_tensor(h_full[:, t % 4, at], up_ps[t % 2][:, at],
                                                  bias_b[:, 2 + c, t:t + 1], h_act[:, t % 2, at],
                                                  ALU.add, ALU.mult)
                last.then_inc(prod_done, 1)
                q = UNITS_ROUTED + t + 3
                at_gate_up = slab_of(dve, q) if q < PREPS else None
                lo_h(u - 1, (u - 1) % 4)
                if t < DVE_ROUNDS:
                    round_down(UNITS_ROUTED + t + 1, down_at[t])
                if t == ACC_AT:
                    add_acc(B - 1, S, T0)
                if t == ACC_AT + 1:
                    round_x3(B - 1)
                if 4 <= t < 4 + POOL_SUMS[0]:
                    finish(t - 4)
                if q < PREPS:
                    lo_gate_up(q, q % W_SLOTS, at_gate_up, GU_DVE_L3)
            t = B - 1
            u = T0 + t
            full_slot_free(u)
            for c in range(2):
                dve.wait_ge(act_done, T0 + 2 * t + c + 1)
                dve.wait_ge(up_ready, u + 1 + c)
                at = slice(c * S, (c + 1) * S)
                V.scalar_tensor_tensor(h_full[:, t % 4, at], last_up[c], bias_b[:, 2 + c, t:t + 1],
                                       h_act[:, t % 2, at], ALU.add, ALU.mult).then_inc(prod_done, 1)
                if c == 0:
                    lo_h(u - 1, (u - 1) % 4)
            dve.wait_ge(acc_read, ACC_BIAS + PAIRS + B + 4)
            finish(4)
            for c in range(2):
                dve.wait_ge(h_hi_done, u + 1 + c)
                h = slice(c * S, (c + 1) * S)
                V.tensor_tensor(h_lo[:, t % 4, h], h_full[:, t % 4, h], h_hi[:, t % 4, h].bitcast(F32),
                                ALU.subtract).then_inc(h_lo_done, 1)
            for t in range(5, B):
                finish(t)


def constants():
    p = np.arange(P)
    c = np.zeros((P, C_COLS), np.float32)
    c[:, C_BLOCK:C_BLOCK + E] = p[:, None] // RANK == np.arange(E)
    c[:, C_DELTA:C_DELTA + RANK] = p[:, None] % RANK == np.arange(RANK)
    c[:, C_RANK:C_RANK + E] = E - np.arange(E)
    c[:, C_IDENT:] = np.eye(P)
    return c


def kernel(x, cond_8, L0_cond_weight, L0_cond_mask, L0_cond_bias, L1_cond_W_base, L1_cond_b_base,
           L1_cond_As, L1_cond_Bs, L2_cond_skill_gate, L2_cond_skill_up, L2_cond_skill_down,
           L2_cond_shared_gate, L2_cond_shared_up, L2_cond_shared_down, L3_cond_W_up, L3_cond_b_up,
           L3_cond_W_gate, L3_cond_b_gate, L3_cond_W_down, L3_cond_b_down):
    import concourse.bacc as bacc
    from concourse.bass_utils import run_bass_kernel_spmd

    a = np.asarray
    cat = np.concatenate

    def moe_slabs(gate, up, down):
        n = gate.shape[0]
        cols = [w.reshape(n, D, HALVES, 256).transpose(1, 0, 2, 3) for w in (gate, up)]
        rows = down.reshape(n, HALVES, 2, P, D).transpose(3, 0, 1, 2, 4).reshape(P, n, HALVES, 2 * D)
        return cat([*cols, rows], axis=3).reshape(P, n * HALVES * SLAB)

    up3, gate3 = (a(w).transpose(2, 0, 1) for w in (L3_cond_W_up, L3_cond_W_gate))
    down3 = a(L3_cond_W_down).transpose(2, 0, 1).reshape(2, P, E, D).transpose(1, 2, 0, 3).reshape(P, E, 2 * D)
    slabs = cat([
        moe_slabs(a(L2_cond_skill_gate), a(L2_cond_skill_up), a(L2_cond_skill_down)),
        cat([up3, gate3, down3], axis=2).reshape(P, E * SLAB),
        moe_slabs(a(L2_cond_shared_gate)[None], a(L2_cond_shared_up)[None], a(L2_cond_shared_down)[None]),
    ], axis=1)
    w_l0 = a(L0_cond_weight).reshape(E, D, TBLK, RANK).transpose(0, 3, 2, 1).reshape(P, TBLK, D)
    lin = np.stack([a(L0_cond_mask), a(L1_cond_As).reshape(P, D),
                    a(L1_cond_Bs).transpose(0, 2, 1).reshape(P, D), a(L1_cond_W_base).T], axis=1)
    chunks = [a(v).reshape(E, 2, P).transpose(2, 1, 0).reshape(P, 2 * E) for v in (L3_cond_b_up, L3_cond_b_gate)]
    vecs = cat([a(L0_cond_bias)[:, None], a(L1_cond_b_base)[:, None], *chunks, a(L3_cond_b_down).T], axis=1)
    data = {
        "xT": a(x).transpose(2, 0, 1).reshape(P, TOKENS), "cond": a(cond_8), "consts": constants(),
        "w_l0": w_l0, "lin": lin, "vecs": vecs, "l0_bias": a(L0_cond_bias), "slabs": slabs,
    }
    data = {k: np.ascontiguousarray(v) for k, v in data.items()}

    nc = bacc.Bacc("TRN2", target_bir_lowering=False, num_devices=1)
    args = {k: nc.dram_tensor(k, v.shape, F32, kind="ExternalInput").ap() for k, v in data.items()}
    outT = nc.dram_tensor("outT", (P, TOKENS), F32, kind="ExternalOutput").ap()
    build(nc, outT=outT, **args)
    r = run_bass_kernel_spmd(nc, [data], core_ids=[0])
    got = r.results[0]["outT"]
    return np.ascontiguousarray(got.reshape(P, B, S).transpose(1, 2, 0))
```
